# Optimizing a Trainium2 kernel written in Bass

```python
import numpy as np
import jax
import jax.numpy as jnp

def _softmax(x, axis=-1):
    return jax.nn.softmax(x, axis=axis)

def _gelu(x):
    return jax.nn.gelu(x, approximate=True)

def _silu(x):
    return jax.nn.silu(x)

def _sigmoid(x):
    return jax.nn.sigmoid(x)

def _layernorm(x, axis=-1, eps=1e-05):
    m = jnp.mean(x, axis=axis, keepdims=True)
    v = jnp.var(x, axis=axis, keepdims=True)
    return (x - m) / jnp.sqrt(v + eps)

def _scatter_add(tgt, idx, src, axis=0):
    return tgt.at[idx].add(src)

def _segment_sum(src, seg, n):
    return jax.ops.segment_sum(src, seg, n)
kernel_name = 'mk_dlrm_tower_d1_rec_r8_a2a0cf'

def setup_inputs(seed: int=0):
    np.random.seed(seed)
    _w = jnp.asarray

    def _rec_inputs():
        import jax
        import jax.numpy as jnp
        _tk = jax.random.key(seed)
        dense_ctx = jax.random.normal(jax.random.fold_in(_tk, 190), (2048, 16), jnp.float32)
        ids = jnp.stack([jax.random.randint(jax.random.fold_in(_tk, 200 + f), (2048,), 0, v, jnp.int32) for f, v in enumerate([12500, 1250, 125000, 1000, 1000, 1250, 125000, 1250, 12500, 1000, 125000, 1250, 125000, 125000, 1000, 1250, 125000, 1250, 125000, 125000, 125000, 1000, 125000, 1250, 125000, 12500, 1250, 1000, 1000, 1000, 1000, 1250])], axis=1)
        tbl_0 = 0.05 * jax.random.normal(jax.random.fold_in(_tk, 500 + 0), (12500, 16), jnp.float32)
        tbl_1 = 0.05 * jax.random.normal(jax.random.fold_in(_tk, 500 + 1), (1250, 16), jnp.float32)
        tbl_2 = 0.05 * jax.random.normal(jax.random.fold_in(_tk, 500 + 2), (125000, 16), jnp.float32)
        tbl_3 = 0.05 * jax.random.normal(jax.random.fold_in(_tk, 500 + 3), (1000, 16), jnp.float32)
        tbl_4 = 0.05 * jax.random.normal(jax.random.fold_in(_tk, 500 + 4), (1000, 16), jnp.float32)
        tbl_5 = 0.05 * jax.random.normal(jax.random.fold_in(_tk, 500 + 5), (1250, 16), jnp.float32)
        tbl_6 = 0.05 * jax.random.normal(jax.random.fold_in(_tk, 500 + 6), (125000, 16), jnp.float32)
        tbl_7 = 0.05 * jax.random.normal(jax.random.fold_in(_tk, 500 + 7), (1250, 16), jnp.float32)
        tbl_8 = 0.05 * jax.random.normal(jax.random.fold_in(_tk, 500 + 8), (12500, 16), jnp.float32)
        tbl_9 = 0.05 * jax.random.normal(jax.random.fold_in(_tk, 500 + 9), (1000, 16), jnp.float32)
        tbl_10 = 0.05 * jax.random.normal(jax.random.fold_in(_tk, 500 + 10), (125000, 16), jnp.float32)
        tbl_11 = 0.05 * jax.random.normal(jax.random.fold_in(_tk, 500 + 11), (1250, 16), jnp.float32)
        tbl_12 = 0.05 * jax.random.normal(jax.random.fold_in(_tk, 500 + 12), (125000, 16), jnp.float32)
        tbl_13 = 0.05 * jax.random.normal(jax.random.fold_in(_tk, 500 + 13), (125000, 16), jnp.float32)
        tbl_14 = 0.05 * jax.random.normal(jax.random.fold_in(_tk, 500 + 14), (1000, 16), jnp.float32)
        tbl_15 = 0.05 * jax.random.normal(jax.random.fold_in(_tk, 500 + 15), (1250, 16), jnp.float32)
        tbl_16 = 0.05 * jax.random.normal(jax.random.fold_in(_tk, 500 + 16), (125000, 16), jnp.float32)
        tbl_17 = 0.05 * jax.random.normal(jax.random.fold_in(_tk, 500 + 17), (1250, 16), jnp.float32)
        tbl_18 = 0.05 * jax.random.normal(jax.random.fold_in(_tk, 500 + 18), (125000, 16), jnp.float32)
        tbl_19 = 0.05 * jax.random.normal(jax.random.fold_in(_tk, 500 + 19), (125000, 16), jnp.float32)
        tbl_20 = 0.05 * jax.random.normal(jax.random.fold_in(_tk, 500 + 20), (125000, 16), jnp.float32)
        tbl_21 = 0.05 * jax.random.normal(jax.random.fold_in(_tk, 500 + 21), (1000, 16), jnp.float32)
        tbl_22 = 0.05 * jax.random.normal(jax.random.fold_in(_tk, 500 + 22), (125000, 16), jnp.float32)
        tbl_23 = 0.05 * jax.random.normal(jax.random.fold_in(_tk, 500 + 23), (1250, 16), jnp.float32)
        tbl_24 = 0.05 * jax.random.normal(jax.random.fold_in(_tk, 500 + 24), (125000, 16), jnp.float32)
        tbl_25 = 0.05 * jax.random.normal(jax.random.fold_in(_tk, 500 + 25), (12500, 16), jnp.float32)
        tbl_26 = 0.05 * jax.random.normal(jax.random.fold_in(_tk, 500 + 26), (1250, 16), jnp.float32)
        tbl_27 = 0.05 * jax.random.normal(jax.random.fold_in(_tk, 500 + 27), (1000, 16), jnp.float32)
        tbl_28 = 0.05 * jax.random.normal(jax.random.fold_in(_tk, 500 + 28), (1000, 16), jnp.float32)
        tbl_29 = 0.05 * jax.random.normal(jax.random.fold_in(_tk, 500 + 29), (1000, 16), jnp.float32)
        tbl_30 = 0.05 * jax.random.normal(jax.random.fold_in(_tk, 500 + 30), (1000, 16), jnp.float32)
        tbl_31 = 0.05 * jax.random.normal(jax.random.fold_in(_tk, 500 + 31), (1250, 16), jnp.float32)
        _rk = jax.random.fold_in(_tk, 7)
        W_top1 = 0.0693375 * jax.random.normal(jax.random.fold_in(_tk, 801), (208, 512), jnp.float32)
        W_top2 = 0.0441942 * jax.random.normal(jax.random.fold_in(_tk, 802), (512, 256), jnp.float32)
        W_top3 = 0.0625 * jax.random.normal(jax.random.fold_in(_tk, 803), (256, 1), jnp.float32)
        b_top1 = jnp.zeros((512,), jnp.float32)
        b_top2 = jnp.zeros((256,), jnp.float32)
        return (dense_ctx, ids, tbl_0, tbl_1, tbl_2, tbl_3, tbl_4, tbl_5, tbl_6, tbl_7, tbl_8, tbl_9, tbl_10, tbl_11, tbl_12, tbl_13, tbl_14, tbl_15, tbl_16, tbl_17, tbl_18, tbl_19, tbl_20, tbl_21, tbl_22, tbl_23, tbl_24, tbl_25, tbl_26, tbl_27, tbl_28, tbl_29, tbl_30, tbl_31, W_top1, b_top1, W_top2, b_top2, W_top3)
    dense_ctx, ids, tbl_0, tbl_1, tbl_2, tbl_3, tbl_4, tbl_5, tbl_6, tbl_7, tbl_8, tbl_9, tbl_10, tbl_11, tbl_12, tbl_13, tbl_14, tbl_15, tbl_16, tbl_17, tbl_18, tbl_19, tbl_20, tbl_21, tbl_22, tbl_23, tbl_24, tbl_25, tbl_26, tbl_27, tbl_28, tbl_29, tbl_30, tbl_31, W_top1, b_top1, W_top2, b_top2, W_top3 = _rec_inputs()

    def _L0_rec_setup():
        import jax, jax.numpy as jnp
        import numpy as np
        B, M, D = (2048, 32, 16)
        LAYERS = [64, 64, 64]
        key = jax.random.key(seed)
        ks = jax.random.split(key, 4)
        inp = {'embeddings': jax.random.normal(ks[0], (B, M, D), dtype=jnp.float32)}
        hk_1 = M
        for i, hk in enumerate(LAYERS):
            scale = (2.0 / (M * hk_1 + hk)) ** 0.5
            inp[f'W{i}'] = jax.random.normal(ks[i + 1], (M, hk_1, hk), dtype=jnp.float32) * scale
            hk_1 = hk
        return inp
    _L0_rec_all = _L0_rec_setup()
    _L0_rec_in = {k: v for k, v in _L0_rec_all.items() if k in ('W0', 'W1', 'W2')}
    del _L0_rec_all
    return {'dense_ctx': dense_ctx, 'ids': ids, 'tbl_0': tbl_0, 'tbl_1': tbl_1, 'tbl_2': tbl_2, 'tbl_3': tbl_3, 'tbl_4': tbl_4, 'tbl_5': tbl_5, 'tbl_6': tbl_6, 'tbl_7': tbl_7, 'tbl_8': tbl_8, 'tbl_9': tbl_9, 'tbl_10': tbl_10, 'tbl_11': tbl_11, 'tbl_12': tbl_12, 'tbl_13': tbl_13, 'tbl_14': tbl_14, 'tbl_15': tbl_15, 'tbl_16': tbl_16, 'tbl_17': tbl_17, 'tbl_18': tbl_18, 'tbl_19': tbl_19, 'tbl_20': tbl_20, 'tbl_21': tbl_21, 'tbl_22': tbl_22, 'tbl_23': tbl_23, 'tbl_24': tbl_24, 'tbl_25': tbl_25, 'tbl_26': tbl_26, 'tbl_27': tbl_27, 'tbl_28': tbl_28, 'tbl_29': tbl_29, 'tbl_30': tbl_30, 'tbl_31': tbl_31, 'W_top1': W_top1, 'b_top1': b_top1, 'W_top2': W_top2, 'b_top2': b_top2, 'W_top3': W_top3, 'L0_rec_W0': _L0_rec_in['W0'], 'L0_rec_W1': _L0_rec_in['W1'], 'L0_rec_W2': _L0_rec_in['W2']}

def reference(dense_ctx, ids, tbl_0, tbl_1, tbl_2, tbl_3, tbl_4, tbl_5, tbl_6, tbl_7, tbl_8, tbl_9, tbl_10, tbl_11, tbl_12, tbl_13, tbl_14, tbl_15, tbl_16, tbl_17, tbl_18, tbl_19, tbl_20, tbl_21, tbl_22, tbl_23, tbl_24, tbl_25, tbl_26, tbl_27, tbl_28, tbl_29, tbl_30, tbl_31, W_top1, b_top1, W_top2, b_top2, W_top3, L0_rec_W0, L0_rec_W1, L0_rec_W2):
    import jax
    import jax.numpy as jnp

    def _L0_rec_ref(embeddings, W0, W1, W2):
        import jax, jax.numpy as jnp
        import numpy as np
        B, M, D = (2048, 32, 16)
        LAYERS = [64, 64, 64]
        x0 = embeddings
        xk = x0
        outs = []
        for W in (W0, W1, W2):
            xk = jax.nn.relu(jnp.einsum('bmd,bhd,mhk->bkd', x0, xk, W))
            outs.append(jnp.sum(xk, axis=2))
        return jnp.concatenate(outs, axis=1)
    e = jnp.stack([tbl_0[ids[:, 0]], tbl_1[ids[:, 1]], tbl_2[ids[:, 2]], tbl_3[ids[:, 3]], tbl_4[ids[:, 4]], tbl_5[ids[:, 5]], tbl_6[ids[:, 6]], tbl_7[ids[:, 7]], tbl_8[ids[:, 8]], tbl_9[ids[:, 9]], tbl_10[ids[:, 10]], tbl_11[ids[:, 11]], tbl_12[ids[:, 12]], tbl_13[ids[:, 13]], tbl_14[ids[:, 14]], tbl_15[ids[:, 15]], tbl_16[ids[:, 16]], tbl_17[ids[:, 17]], tbl_18[ids[:, 18]], tbl_19[ids[:, 19]], tbl_20[ids[:, 20]], tbl_21[ids[:, 21]], tbl_22[ids[:, 22]], tbl_23[ids[:, 23]], tbl_24[ids[:, 24]], tbl_25[ids[:, 25]], tbl_26[ids[:, 26]], tbl_27[ids[:, 27]], tbl_28[ids[:, 28]], tbl_29[ids[:, 29]], tbl_30[ids[:, 30]], tbl_31[ids[:, 31]]], axis=1)
    z = _L0_rec_ref(e, L0_rec_W0, L0_rec_W1, L0_rec_W2)
    z = z.reshape(z.shape[0], -1)
    h = jnp.concatenate([z, dense_ctx], axis=1)
    h = jnp.maximum(h @ W_top1 + b_top1, 0.0)
    h = jnp.maximum(h @ W_top2 + b_top2, 0.0)
    y = h @ W_top3
    return y

_drawn_inputs = setup_inputs


def setup_inputs(seed=0):
    import zlib

    import numpy as np

    out = dict(_drawn_inputs(seed))
    spreads = {'b_top1': (0.0, 2.0), 'b_top2': (0.0, 0.8)}
    factors = {'tbl_0': 8.0,
     'tbl_1': 8.0,
     'tbl_2': 8.0,
     'tbl_3': 8.0,
     'tbl_4': 8.0,
     'tbl_5': 8.0,
     'tbl_6': 8.0,
     'tbl_7': 8.0,
     'tbl_8': 8.0,
     'tbl_9': 8.0,
     'tbl_10': 8.0,
     'tbl_11': 8.0,
     'tbl_12': 8.0,
     'tbl_13': 8.0,
     'tbl_14': 8.0,
     'tbl_15': 8.0,
     'tbl_16': 8.0,
     'tbl_17': 8.0,
     'tbl_18': 8.0,
     'tbl_19': 8.0,
     'tbl_20': 8.0,
     'tbl_21': 8.0,
     'tbl_22': 8.0,
     'tbl_23': 8.0,
     'tbl_24': 8.0,
     'tbl_25': 8.0,
     'tbl_26': 8.0,
     'tbl_27': 8.0,
     'tbl_28': 8.0,
     'tbl_29': 8.0,
     'tbl_30': 8.0,
     'tbl_31': 8.0,
     'L0_rec_W0': 3.554,
     'L0_rec_W1': 8.0,
     'L0_rec_W2': 8.0,
     'dense_ctx': 7.615}
    for name, (base, spread) in spreads.items():
        noise = np.random.default_rng([zlib.crc32(name.encode()), seed]).standard_normal(out[name].shape)
        drawn = base * np.exp(spread * noise) if base else spread * noise
        out[name] = jnp.asarray(drawn.astype(out[name].dtype))
    for name, factor in factors.items():
        out[name] = (out[name] * factor).astype(out[name].dtype)
    return out
```

```python
from contextlib import ExitStack

import concourse.bass as bass
from concourse import mybir

F32 = mybir.dt.float32
I32 = mybir.dt.int32
ALU = mybir.AluOpType
ACT = mybir.ActivationFunctionType
AX = mybir.AxisListType

P = 128
B, M, D, H = 2048, 32, 16, 64
G = B // P
N = 512
DC = N // P
CHUNKS = D // DC
PAIRS = CHUNKS // 2
MQ = M // 4
HH = H // 32
KT = MQ * HH
ZU = 4
BLOCKS = KT // ZU
ZS = 2 * BLOCKS
T0 = 4
XS = 4
LG = 2 * PAIRS
ZPG = LG * ZS
UPG = LG * BLOCKS
XPG = LG * 2 * HH
ROWS = 3 * M
F1, F2 = 512, 256
DMA = 16

ACC0, ACC1, ACC2 = (0, 1), (2, 0), (1, 2)


def build(nc, dense_t, ids, tables, w0_a, w0_b, w0_diag, w1, w2, wt1_cin, wt1_dense, bt1, wt2, bt2, wt3, out):
    x0_dram = nc.dram_tensor("x0_scratch", [CHUNKS, ROWS, N], F32, kind="Internal").ap()
    ctx = ExitStack()
    with ctx:
        def sb(name, shape, dt=F32):
            return ctx.enter_context(nc.sbuf_tensor(name, shape, dt))

        def sem(name):
            return ctx.enter_context(nc.semaphore(name))

        ident = sb("ident", [P, P])
        idx = sb("idx", [P, M], I32)
        looked_up = sb("looked_up", [P, M * D])
        x0_t = sb("x0_t", [P, CHUNKS, P])
        x0_sq = sb("x0_sq", [P, CHUNKS, P])
        x0_b = sb("x0_b", [P, CHUNKS, MQ, N])
        l0_rep = sb("l0_rep", [P, 2, N])
        l0_z = sb("l0_z", [P, 2, T0, N])
        l0_sq = sb("l0_sq", [P, 2, N])
        z = sb("z", [P, ZS, ZU, N])
        w0_s = sb("w0_s", [P, T0, H])
        w0_t = sb("w0_t", [P, T0, H])
        w0_d = sb("w0_d", [P, H])
        w_cin = sb("w_cin", [P, 2, KT, H])
        wt1_c = sb("wt1_c", [P, 3, F1])
        wt1_d = sb("wt1_d", [D, F1])
        wt2_s = sb("wt2_s", [P, F1 // P, F2])
        wt3_s = sb("wt3_s", [P, F2 // P])
        bt1_s = sb("bt1_s", [P, F1 // P])
        bt2_s = sb("bt2_s", [P, F2 // P])
        zsum = sb("zsum", [P, 3, DC, P])
        zvec = sb("zvec", [P, 3, P])
        dense_s = sb("dense_s", [D, P])
        h1 = sb("h1", [P, F1 // P, P])
        h2 = sb("h2", [P, F2 // P, P])
        y_s = sb("y_s", [1, B])

        acc = ctx.enter_context(nc.psum_tensor("acc", [P, 3, N], F32))
        xk = ctx.enter_context(nc.psum_tensor("xk", [P, XS, N], F32))
        stage = ctx.enter_context(nc.psum_tensor("stage", [P, N], F32))

        weights_loaded = sem("weights_loaded")
        padding_zero = sem("padding_zero")
        ident_zero = sem("ident_zero")
        ident_ready = sem("ident_ready")
        w0_ready = sem("w0_ready")
        idx_loaded = sem("idx_loaded")
        rows_looked_up = sem("rows_looked_up")
        x0_transposed = sem("x0_transposed")
        x0_in_sbuf = sem("x0_in_sbuf")
        x0_stored = sem("x0_stored")
        l0_loaded = [sem(f"l0_loaded{c}") for c in range(2)]
        x0b_loaded = [sem(f"x0b_loaded{c}") for c in range(CHUNKS)]
        l0_products = sem("l0_products")
        l0_done = sem("l0_done")
        xk_ready = sem("xk_ready")
        z_ready = sem("z_ready")
        z_used = sem("z_used")
        acc_summed = sem("acc_summed")
        zvec_ready = sem("zvec_ready")
        dense_loaded = sem("dense_loaded")
        h1_done = sem("h1_done")
        h1_ready = sem("h1_ready")
        h2_done = sem("h2_done")
        h2_ready = sem("h2_ready")
        y_done = sem("y_done")
        y_ready = sem("y_ready")
        out_stored = sem("out_stored")
        steps_of_sync = sem("steps_of_sync")

        weight_loads = [
            (w0_s, w0_a), (w0_t, w0_b), (w_cin[:, 0], w1), (w_cin[:, 1], w2), (wt1_c, wt1_cin),
            (wt2_s, wt2), (wt3_s, wt3), (bt1_s, bt1), (bt2_s, bt2),
        ]
        WEIGHTS = DMA * (len(weight_loads) + 2)
        L0_LOADS = 9
        X0B_LOADS = 4

        def z_block(s, j, c):
            return ZS * s + 2 * j + c

        block = ctx.enter_context(nc.Block())

        @block.sync
        def _(sp):
            def load_idx(g):
                sp.dma_start(idx[:], ids[bass.ds(g, 1)].rearrange("g r m -> (g r) m")).then_inc(idx_loaded, DMA)

            def store_x0():
                for first, src in ((0, x0_t), (M, x0_t), (2 * M, x0_sq)):
                    dst = x0_dram[:, first:first + M, :].rearrange("q m (c r) -> (m c) q r", c=DC)
                    sp.dma_start(dst, src[:]).then_inc(x0_stored, DMA)

            def load_l0(pair):
                for c in range(2):
                    rows = x0_dram[2 * pair + c]
                    for j in range(4):
                        part = slice(32 * j, 32 * j + 32)
                        shifted = rows[j + 1:j + 1 + M, :]
                        src = bass.AP(shifted.tensor, shifted.offset, [[N, M], [4 * N, T0], [1, N]])
                        sp.dma_start(l0_z[part, c], src).then_inc(l0_loaded[c], DMA)
                        sp.dma_start(l0_rep[part, c], rows[0:M, :]).then_inc(l0_loaded[c], DMA)
                    sp.dma_start(l0_sq[0:M, c], rows[2 * M:ROWS, :]).then_inc(l0_loaded[c], DMA)

            def load_x0b(c):
                rows = x0_dram[c]
                for j in range(4):
                    first = rows[j:j + 1, :]
                    src = bass.AP(first.tensor, first.offset, [[0, 32], [4 * N, MQ], [1, N]])
                    sp.dma_start(x0_b[32 * j:32 * j + 32, c], src).then_inc(x0b_loaded[c], DMA)

            def load_dense(g):
                sp.dma_start(dense_s[:], dense_t[bass.ds(g, 1)].rearrange("g d r -> (g d) r")).then_inc(dense_loaded, DMA)

            def iteration(g, front, lookup, mlp):
                def wait(semaphore, value):
                    sp.wait_ge(semaphore, value)
                    sp.sem_inc(steps_of_sync, 1)

                if mlp:
                    wait(h1_done, g)
                load_dense(g)
                if not front:
                    return
                for c in range(2):
                    wait(l0_loaded[c], 2 * L0_LOADS * DMA * (g + 1))
                for c in range(CHUNKS):
                    wait(x0b_loaded[c], X0B_LOADS * DMA * (g + 1))
                wait(x0_in_sbuf, 2 * g + 4)
                store_x0()
                wait(x0_stored, 3 * DMA * (g + 2))
                wait(l0_done, 2 * g + 2)
                load_l0(0)
                for c in range(2):
                    wait(z_ready, ZPG * g + z_block(2, BLOCKS - 1, c) + 1)
                    load_x0b(c)
                wait(l0_done, 2 * g + 3)
                load_l0(1)
                for c in range(2):
                    wait(z_ready, ZPG * g + z_block(3, BLOCKS - 1, c) + 1)
                    load_x0b(2 + c)
                if lookup is not None:
                    wait(rows_looked_up, M * DMA * (g + 3))
                    if lookup:
                        load_idx(g + 3)

            load_idx(0)
            for dst, src in weight_loads:
                sp.dma_start(dst[:] if dst.shape[0] == P else dst, src).then_inc(weights_loaded, DMA)
            sp.wait_ge(padding_zero, 2)
            sp.dma_start(w0_d[0:M, :], w0_diag).then_inc(weights_loaded, DMA)
            sp.dma_start(wt1_d[:], wt1_dense).then_inc(weights_loaded, DMA)
            sp.wait_ge(rows_looked_up, M * DMA)
            load_idx(1)
            sp.wait_ge(x0_in_sbuf, 2)
            store_x0()
            sp.wait_ge(x0_stored, 3 * DMA)
            load_l0(0)
            load_x0b(0)
            load_x0b(1)
            sp.wait_ge(l0_done, 1)
            load_l0(1)
            load_x0b(2)
            load_x0b(3)
            sp.wait_ge(rows_looked_up, 2 * M * DMA)
            load_idx(2)
            iteration(0, True, True, False)
            with sp.Fori(1, G - 3) as g:
                iteration(g, True, True, True)
            iteration(G - 3, True, False, True)
            iteration(G - 2, True, None, True)
            iteration(G - 1, False, None, True)
            sp.wait_ge(y_ready, G)
            sp.dma_start(out.rearrange("b one -> one b"), y_s[0:1, :]).then_inc(out_stored, DMA)
            sp.wait_ge(out_stored, DMA)

        @block.gpsimd
        def _(pool):
            def look_up(fields):
                for m in fields:
                    pool.indirect_dma_start(
                        out=looked_up[:, m * D:(m + 1) * D], out_offset=None, in_=tables[m],
                        in_offset=bass.IndirectOffsetOnAxis(ap=idx[:, m:m + 1], axis=0),
                    ).then_inc(rows_looked_up, DMA)

            def products(g, pair):
                for c in range(2):
                    pool.wait_ge(l0_loaded[c], L0_LOADS * DMA * (2 * g + pair + 1))
                    nc.gpsimd.tensor_tensor(
                        l0_z[:, c], l0_z[:, c], l0_rep[:, c].unsqueeze(1).to_broadcast([P, T0, N]), ALU.mult,
                    ).then_inc(l0_products, 1)

            def iteration(g, lookup):
                if lookup:
                    pool.wait_ge(idx_loaded, DMA * (g + 3))
                    pool.wait_ge(x0_transposed, g + 2)
                products(g + 1, 0)
                if lookup:
                    look_up(range(0, M // 2))
                products(g + 1, 1)
                if lookup:
                    look_up(range(M // 2, M))

            nc.gpsimd.memset(ident[:], 0.0).then_inc(ident_zero, 1)
            pool.wait_ge(ident_zero, 1)
            nc.gpsimd.affine_select(
                out=ident[:], in_=ident[:], compare_op=ALU.not_equal, fill=1.0, base=0,
                pattern=[[-1, P]], channel_multiplier=1,
            ).then_inc(ident_ready, 1)
            pool.wait_ge(idx_loaded, DMA)
            look_up(range(M))
            products(0, 0)
            pool.wait_ge(x0_transposed, 1)
            pool.wait_ge(idx_loaded, 2 * DMA)
            products(0, 1)
            look_up(range(M))
            with pool.Fori(0, G - 2) as g:
                iteration(g, True)
            iteration(G - 2, False)

        @block.tensor
        def _(pe):
            def transposes(g):
                pe.wait_ge(rows_looked_up, M * DMA * (g + 1))
                by_coord = looked_up[:].rearrange("p (mc q) -> p q mc", q=CHUNKS)
                for q in range(CHUNKS):
                    last = nc.tensor.transpose(stage[:, q * P:(q + 1) * P], by_coord[:, q], ident[:])
                last.then_inc(x0_transposed, 1)

            def layer0(g, pair):
                to = acc[:, ACC0[pair]]
                pe.wait_ge(l0_products, 4 * g + 2 * pair + 2)
                for t in range(T0):
                    for c in range(2):
                        nc.tensor.matmul(to[64 * c:64 * c + H], w0_s[:, t], l0_z[:, c, t], start=(t == 0), stop=False)
                for c in range(2):
                    last = nc.tensor.matmul(to[64 * c:64 * c + H], w0_d[:], l0_sq[:, c], start=False, stop=True)
                last.then_inc(l0_done, 1)

            def contract(g, s):
                layer, pair = 1 + s // PAIRS, s % PAIRS
                to = acc[:, (ACC0, ACC1, ACC2)[layer][pair]]
                for j in range(BLOCKS):
                    pe.wait_ge(z_ready, ZPG * g + z_block(s, j, 1) + 1)
                    for u in range(ZU):
                        k = j * ZU + u
                        for c in range(2):
                            last = nc.tensor.matmul(
                                to[64 * c:64 * c + H], w_cin[:, layer - 1, k], z[:, 2 * j + c, u],
                                start=(k == 0), stop=(k == KT - 1),
                            )
                    last.then_inc(z_used, 1)

            def mlp1(g, staged):
                pe.wait_ge(zvec_ready, g + 1)
                pe.wait_ge(dense_loaded, DMA * (g + 1))
                pe.wait_ge(x0_in_sbuf, 2 * staged)
                for i in range(F1 // P):
                    cols = slice(i * P, (i + 1) * P)
                    for layer in range(3):
                        nc.tensor.matmul(stage[:, cols], wt1_c[:, layer, cols], zvec[:, layer], start=(layer == 0), stop=False)
                    last = nc.tensor.matmul(stage[:, cols], wt1_d[:, cols], dense_s[:], start=False, stop=True)
                last.then_inc(h1_done, 1)

            def mlp2(g):
                pe.wait_ge(h1_ready, g + 1)
                for i in range(F2 // P):
                    cols = slice(i * P, (i + 1) * P)
                    for k in range(F1 // P):
                        last = nc.tensor.matmul(stage[:, cols], wt2_s[:, k, cols], h1[:, k], start=(k == 0), stop=(k == F1 // P - 1))
                last.then_inc(h2_done, 1)

            def mlp3(g):
                pe.wait_ge(h2_ready, g + 1)
                for k in range(F2 // P):
                    last = nc.tensor.matmul(stage[0:1, 0:P], wt3_s[:, k:k + 1], h2[:, k], start=(k == 0), stop=(k == F2 // P - 1))
                last.then_inc(y_done, 1)

            def iteration(g, front, mlp):
                if mlp:
                    pe.wait_ge(acc_summed, 6 * g)
                contract(g, 0)
                if mlp:
                    mlp1(g - 1, g + 1)
                pe.wait_ge(xk_ready, XPG * g + 4)
                pe.wait_ge(acc_summed, 6 * g + 1)
                contract(g, 1)
                if mlp:
                    mlp2(g - 1)
                pe.wait_ge(xk_ready, XPG * g + 8)
                pe.wait_ge(acc_summed, 6 * g + 2)
                contract(g, 2)
                if mlp:
                    mlp3(g - 1)
                if front:
                    if mlp:
                        pe.wait_ge(y_ready, g)
                    transposes(g + 1)
                    pe.wait_ge(xk_ready, XPG * g + 16)
                    pe.wait_ge(acc_summed, 6 * g + 4)
                    layer0(g + 1, 0)
                pe.wait_ge(xk_ready, XPG * g + 12)
                pe.wait_ge(acc_summed, 6 * g + 3)
                contract(g, 3)
                if front:
                    pe.wait_ge(acc_summed, 6 * g + 5)
                    layer0(g + 1, 1)

            pe.wait_ge(ident_ready, 1)
            transposes(0)
            pe.wait_ge(w0_ready, 2)
            pe.wait_ge(weights_loaded, WEIGHTS)
            layer0(0, 0)
            layer0(0, 1)
            iteration(0, True, False)
            with pe.Fori(1, G - 1) as g:
                iteration(g, True, True)
            iteration(G - 1, False, True)
            pe.wait_ge(y_ready, G - 1)
            mlp1(G - 1, G)
            mlp2(G - 1)
            mlp3(G - 1)

        @block.scalar
        def _(act):
            def x0_out(g):
                act.wait_ge(x0_transposed, g + 1)
                if not (isinstance(g, int) and g == 0):
                    act.wait_ge(x0_stored, 3 * DMA * g)
                src = stage[:].rearrange("p (q r) -> p q r", q=CHUNKS)
                nc.scalar.activation(x0_t[:], src, ACT.Copy).then_inc(x0_in_sbuf, 1)
                nc.scalar.activation(x0_sq[:], src, ACT.Square).then_inc(x0_in_sbuf, 1)

            def xk_tiles(g, s, bank, wait_source, first=False):
                wait_source()
                for h in range(HH):
                    for c in range(2):
                        slot = 2 * h + c
                        if not first:
                            act.wait_ge(z_ready, ZPG * g + z_block(s - 1, 2 * h + 1, c) + 1)
                        src = acc[64 * c + 32 * h:64 * c + 32 * h + 32, bank]
                        for q in range(4):
                            last = nc.scalar.activation(xk[32 * q:32 * q + 32, slot], src, ACT.Relu)
                        last.then_inc(xk_ready, 1)

            def after_layer0(g, pair):
                return lambda: act.wait_ge(l0_done, 2 * g + pair + 1)

            def after_step(g, s):
                return lambda: act.wait_ge(z_used, UPG * g + BLOCKS * (s + 1))

            def h1_out(g):
                act.wait_ge(h1_done, g + 1)
                if not (isinstance(g, int) and g == 0):
                    act.wait_ge(h2_done, g)
                for i in range(F1 // P):
                    last = nc.scalar.activation(h1[:, i], stage[:, i * P:(i + 1) * P], ACT.Relu, bias=bt1_s[:, i:i + 1])
                last.then_inc(h1_ready, 1)

            def h2_out(g):
                act.wait_ge(h2_done, g + 1)
                if not (isinstance(g, int) and g == 0):
                    act.wait_ge(y_done, g)
                for i in range(F2 // P):
                    last = nc.scalar.activation(h2[:, i], stage[:, i * P:(i + 1) * P], ACT.Relu, bias=bt2_s[:, i:i + 1])
                last.then_inc(h2_ready, 1)

            def y_out(g):
                act.wait_ge(y_done, g + 1)
                nc.scalar.activation(y_s[0:1, bass.ds(g * P, P)], stage[0:1, 0:P], ACT.Copy).then_inc(y_ready, 1)

            def iteration(g, front, mlp):
                xk_tiles(g, 1, ACC0[1], after_layer0(g, 1))
                if mlp:
                    h1_out(g - 1)
                xk_tiles(g, 2, ACC1[0], after_step(g, 0))
                if mlp:
                    h2_out(g - 1)
                xk_tiles(g, 3, ACC1[1], after_step(g, 1))
                if mlp:
                    y_out(g - 1)
                if front:
                    x0_out(g + 1)
                    xk_tiles(g, 4, ACC0[0], after_layer0(g + 1, 0))

            x0_out(0)
            act.wait_ge(weights_loaded, WEIGHTS)
            xk_tiles(0, 0, ACC0[0], after_layer0(0, 0), first=True)
            iteration(0, True, False)
            with act.Fori(1, G - 1) as g:
                iteration(g, True, True)
            iteration(G - 1, False, True)
            h1_out(G - 1)
            h2_out(G - 1)
            y_out(G - 1)

        @block.vector
        def _(dve):
            def products(g, s, j, c, fresh):
                chunk, h, m0 = 2 * (s % PAIRS) + c, (j * ZU) // MQ, (j * ZU) % MQ
                if s < PAIRS and j == 0:
                    dve.wait_ge(x0b_loaded[chunk], X0B_LOADS * DMA * (g + 1))
                if j % (BLOCKS // HH) == 0:
                    dve.wait_ge(xk_ready, XPG * g + 2 * HH * s + 2 * h + c + 1)
                if c == 0 and not (fresh and s == 0):
                    dve.wait_ge(z_used, UPG * g + BLOCKS * (s - 1) + j + 1)
                nc.vector.tensor_tensor(
                    z[:, 2 * j + c], x0_b[:, chunk, m0:m0 + ZU],
                    xk[:, 2 * h + c].unsqueeze(1).to_broadcast([P, ZU, N]), ALU.mult,
                ).then_inc(z_ready, 1)

            def add_up(layer, pair, done):
                src = acc[:, (ACC0, ACC1, ACC2)[layer][pair]]
                dst = zsum[:, layer].rearrange("p c r -> p (c r)")
                if pair == 0:
                    ins = nc.vector.tensor_scalar(dst, src, 0.0, None, ALU.max)
                else:
                    dve.wait_ge(acc_summed, done)
                    ins = nc.vector.scalar_tensor_tensor(dst, src, 0.0, dst, ALU.max, ALU.add)
                ins.then_inc(acc_summed, 1)

            def finish(g, fresh=False):
                dve.wait_ge(z_used, UPG * (g + 1))
                add_up(2, 1, 6 * g + 5)
                dve.wait_ge(acc_summed, 6 * g + 6)
                if not fresh:
                    dve.wait_ge(h1_done, g)
                nc.vector.tensor_reduce(zvec[:], zsum[:].rearrange("p l c r -> p l r c"), AX.X, ALU.add).then_inc(zvec_ready, 1)

            def iteration(g, fresh=False, second=False):
                for s in range(LG):
                    for j in range(BLOCKS):
                        for c in range(2):
                            products(g, s, j, c, fresh)
                        if (s, j) == (0, 1):
                            if not fresh:
                                finish(g - 1, second)
                                dve.wait_ge(zvec_ready, g)
                            dve.wait_ge(xk_ready, XPG * g + 4)
                            add_up(0, 0, None)
                        if (s, j) == (0, 3):
                            dve.wait_ge(xk_ready, XPG * g + 8)
                            add_up(0, 1, 6 * g + 1)
                        if (s, j) == (2, 0):
                            dve.wait_ge(xk_ready, XPG * g + 12)
                            add_up(1, 0, None)
                        if (s, j) == (3, 0):
                            dve.wait_ge(xk_ready, XPG * g + 16)
                            add_up(1, 1, 6 * g + 3)
                        if (s, j) == (3, 2):
                            dve.wait_ge(z_used, UPG * g + 3 * BLOCKS)
                            add_up(2, 0, None)

            nc.vector.memset(l0_sq[:], 0.0).then_inc(padding_zero, 1)
            nc.vector.memset(w0_d[:], 0.0).then_inc(padding_zero, 1)
            dve.wait_ge(weights_loaded, WEIGHTS)
            nc.vector.tensor_tensor(w0_s[:, 0:T0 - 1], w0_s[:, 0:T0 - 1], w0_t[:, 0:T0 - 1], ALU.add).then_inc(w0_ready, 1)
            nc.vector.tensor_tensor(w0_s[0:96, T0 - 1], w0_s[0:96, T0 - 1], w0_t[0:96, T0 - 1], ALU.add).then_inc(w0_ready, 1)
            iteration(0, fresh=True)
            iteration(1, second=True)
            with dve.Fori(2, G) as g:
                iteration(g)
            finish(G - 1)


def kernel(dense_ctx, ids, W_top1, b_top1, W_top2, b_top2, W_top3, L0_rec_W0, L0_rec_W1, L0_rec_W2, **tables):
    import concourse.bacc as bacc
    import numpy as np
    from concourse.bass_utils import run_bass_kernel_spmd

    w0 = np.asarray(L0_rec_W0)
    j, m, t = np.meshgrid(np.arange(4), np.arange(M), np.arange(T0), indexing="ij")
    other = (m + 4 * t + j + 1) % M

    def tiles(w):
        w = np.asarray(w).reshape(MQ, 4, HH, 32, H)
        return np.ascontiguousarray(w.transpose(1, 3, 2, 0, 4).reshape(P, KT, H))

    wt1 = np.asarray(W_top1)
    cin = wt1[:3 * H].reshape(3, H, F1)
    arrays = {
        "dense_t": np.ascontiguousarray(np.asarray(dense_ctx).reshape(G, P, D).transpose(0, 2, 1)),
        "ids": np.asarray(ids).reshape(G, P, M),
        "w0_a": np.ascontiguousarray(w0[m, other].reshape(P, T0, H)),
        "w0_b": np.ascontiguousarray(w0[other, m].reshape(P, T0, H)),
        "w0_diag": np.ascontiguousarray(w0[np.arange(M), np.arange(M)]),
        "w1": tiles(L0_rec_W1),
        "w2": tiles(L0_rec_W2),
        "wt1_cin": np.ascontiguousarray(np.concatenate([cin, cin], axis=1).transpose(1, 0, 2)),
        "wt1_dense": np.ascontiguousarray(wt1[3 * H:]),
        "bt1": np.ascontiguousarray(np.asarray(b_top1).reshape(F1 // P, P).T),
        "wt2": np.ascontiguousarray(np.asarray(W_top2).reshape(F1 // P, P, F2).transpose(1, 0, 2)),
        "bt2": np.ascontiguousarray(np.asarray(b_top2).reshape(F2 // P, P).T),
        "wt3": np.ascontiguousarray(np.asarray(W_top3).reshape(F2 // P, P).T),
    }
    for f in range(M):
        arrays[f"tbl_{f}"] = np.asarray(tables[f"tbl_{f}"])
    nc = bacc.Bacc("TRN2", target_bir_lowering=False, num_devices=1)
    dram = {
        name: nc.dram_tensor(name, a.shape, mybir.dt.from_np(a.dtype), kind="ExternalInput").ap()
        for name, a in arrays.items()
    }
    out = nc.dram_tensor("y", (B, 1), F32, kind="ExternalOutput").ap()
    table_aps = [dram.pop(f"tbl_{f}") for f in range(M)]
    build(nc, tables=table_aps, out=out, **dram)
    r = run_bass_kernel_spmd(nc, [arrays], core_ids=[0])
    return r.results[0]["y"]
```

```python
from contextlib import ExitStack

import concourse.bass as bass
from concourse import mybir

F32 = mybir.dt.float32
I32 = mybir.dt.int32
ALU = mybir.AluOpType
ACT = mybir.ActivationFunctionType
AX = mybir.AxisListType

P = 128
B, M, D, H = 2048, 32, 16, 64
G = B // P
N = 512
DC = N // P
CHUNKS = D // DC
PAIRS = CHUNKS // 2
MQ = M // 4
HH = H // 32
KT = MQ * HH
ZU = 4
BLOCKS = KT // ZU
ZS = 2 * BLOCKS
T0 = 4
XS = 4
LG = 2 * PAIRS
BY_POOL = {(s, BLOCKS - 1, 1) for s in range(3)}
ZPG = LG * ZS - len(BY_POOL)
UPG = LG * BLOCKS
XPG = LG * 2 * HH
ROWS = 3 * M
F1, F2 = 512, 256
DMA = 16

ACC0, ACC1, ACC2 = (0, 1), (2, 0), (1, 2)


def build(nc, dense_t, ids, tables, w0_a, w0_b, w0_diag, w1, w2, wt1, bt1, wt2, bt2, wt3, out):
    x0_dram = nc.dram_tensor("x0_scratch", [CHUNKS, ROWS, N], F32, kind="Internal").ap()
    ctx = ExitStack()
    with ctx:
        def sb(name, shape, dt=F32):
            return ctx.enter_context(nc.sbuf_tensor(name, shape, dt))

        def sem(name):
            return ctx.enter_context(nc.semaphore(name))

        ident = sb("ident", [P, P])
        idx = sb("idx", [P, M], I32)
        looked_up = sb("looked_up", [P, M * D])
        x0_t = sb("x0_t", [P, CHUNKS, P])
        x0_sq = sb("x0_sq", [P, CHUNKS, P])
        x0_b = sb("x0_b", [P, CHUNKS, MQ, N])
        xk_pool = sb("xk_pool", [P, N])
        l0_rep = sb("l0_rep", [P, 2, N])
        l0_z = sb("l0_z", [P, CHUNKS, T0, N])
        l0_sq = sb("l0_sq", [PAIRS * M, 2, N])
        z = sb("z", [P, ZS, ZU, N])
        w0_s = sb("w0_s", [P, T0, H])
        w0_t = z[:, 0, 0, 0:T0 * H].rearrange("p (t k) -> p t k", t=T0)
        w0_d = sb("w0_d", [PAIRS * M, H])
        w_cin = sb("w_cin", [P, 2, KT, H])
        wt1_s = sb("wt1_s", [P, 2, F1])
        wt2_s = sb("wt2_s", [P, F1 // P, F2])
        wt3_s = sb("wt3_s", [P, F2 // P])
        bt1_s = sb("bt1_s", [P, F1 // P])
        bt2_s = sb("bt2_s", [P, F2 // P])
        zsum = sb("zsum", [P, DC * P])
        zvec = sb("zvec", [P, 3, P])
        zcross = sb("zcross", [P, 2, P])
        mlp_in = sb("mlp_in", [P, 2, P])
        mlp_zvec = [(0, 0, 0), (1, 64, 0), (2, 0, 1)]
        dense_s = mlp_in[H:H + D, 1]
        h1 = sb("h1", [P, F1 // P, P])
        h2 = sb("h2", [P, F2 // P, P])
        y_s = sb("y_s", [1, P])

        acc = ctx.enter_context(nc.psum_tensor("acc", [P, 3, N], F32))
        xk = ctx.enter_context(nc.psum_tensor("xk", [P, XS, N], F32))
        stage = ctx.enter_context(nc.psum_tensor("stage", [P, N], F32))

        weights_loaded = sem("weights_loaded")
        ident_zero = sem("ident_zero")
        ident_ready = sem("ident_ready")
        w0_ready = sem("w0_ready")
        idx_loaded = sem("idx_loaded")
        rows_looked_up = sem("rows_looked_up")
        x0_transposed = sem("x0_transposed")
        x0_in_sbuf = sem("x0_in_sbuf")
        x0_stored = sem("x0_stored")
        z0_loaded = [sem(f"z0_loaded{p}") for p in range(PAIRS)]
        rep_loaded = sem("rep_loaded")
        x0b_loaded = [sem(f"x0b_loaded{c}") for c in range(CHUNKS)]
        l0_products = sem("l0_products")
        l0_done = sem("l0_done")
        xk_ready = sem("xk_ready")
        xk_pool_ready = sem("xk_pool_ready")
        z_by_pool = sem("z_by_pool")
        z_ready = sem("z_ready")
        z_used = sem("z_used")
        acc_summed = sem("acc_summed")
        zvec_ready = sem("zvec_ready")
        zcross_ready = sem("zcross_ready")
        mlp_in_ready = sem("mlp_in_ready")
        dense_loaded = sem("dense_loaded")
        h1_done = sem("h1_done")
        h1_ready = sem("h1_ready")
        h2_done = sem("h2_done")
        h2_ready = sem("h2_ready")
        y_done = sem("y_done")
        y_ready = sem("y_ready")
        out_stored = sem("out_stored")
        steps_of_sync = sem("steps_of_sync")
        steps_of_pool = sem("steps_of_pool")

        weight_loads = [
            (w0_s, w0_a), (w0_t, w0_b), (w_cin[:, 0], w1), (w_cin[:, 1], w2), (wt1_s[:, 0], wt1[0:P]),
            (wt2_s, wt2), (wt3_s, wt3), (bt1_s, bt1), (bt2_s, bt2),
        ]
        WEIGHTS = DMA * (len(weight_loads) + PAIRS + 1)
        Z0_LOADS = 9
        REP_LOADS = 4
        X0B_LOADS = 4

        def made(s, j, c):
            at = (s, j, c)
            return sum(b <= at and b not in BY_POOL for b in
                       [(i, k, e) for i in range(LG) for k in range(BLOCKS) for e in range(2)])

        def by_pool(s):
            return sum(b[0] <= s for b in BY_POOL)

        block = ctx.enter_context(nc.Block())

        @block.sync
        def _(sp):
            def load_idx(g):
                sp.dma_start(idx[:], ids[bass.ds(g, 1)].rearrange("g r m -> (g r) m")).then_inc(idx_loaded, DMA)

            def store_x0():
                for first, src in ((0, x0_t), (M, x0_t), (2 * M, x0_sq)):
                    dst = x0_dram[:, first:first + M, :].rearrange("q m (c r) -> (m c) q r", c=DC)
                    sp.dma_start(dst, src[:]).then_inc(x0_stored, DMA)

            def load_z0(pair):
                rows = x0_dram[2 * pair:2 * pair + 2]
                for j in range(4):
                    shifted = rows[:, j + 1:j + 1 + M]
                    for c in range(2):
                        src = bass.AP(shifted.tensor, shifted.offset + c * ROWS * N, [[N, M], [4 * N, T0], [1, N]])
                        sp.dma_start(l0_z[32 * j:32 * j + 32, 2 * pair + c], src).then_inc(z0_loaded[pair], DMA)
                sp.dma_start(l0_sq[M * pair:M * pair + M], rows[:, 2 * M:ROWS].rearrange("c m n -> m c n")).then_inc(z0_loaded[pair], DMA)

            def load_rep(pair):
                rows = x0_dram[2 * pair:2 * pair + 2, 0:M].rearrange("c m n -> m c n")
                for j in range(4):
                    sp.dma_start(l0_rep[32 * j:32 * j + 32], rows).then_inc(rep_loaded, DMA)

            def load_x0b(c):
                rows = x0_dram[c]
                for j in range(4):
                    first = rows[j:j + 1, :]
                    src = bass.AP(first.tensor, first.offset, [[0, 32], [4 * N, MQ], [1, N]])
                    sp.dma_start(x0_b[32 * j:32 * j + 32, c], src).then_inc(x0b_loaded[c], DMA)

            def load_dense(g):
                sp.dma_start(dense_s, dense_t[bass.ds(g, 1)].rearrange("g d r -> (g d) r")).then_inc(dense_loaded, DMA)

            def iteration(g, front, lookup, mlp):
                def wait(semaphore, value):
                    sp.wait_ge(semaphore, value)
                    sp.sem_inc(steps_of_sync, 1)

                def dense():
                    if mlp:
                        wait(h1_done, g)
                    load_dense(g)

                if not front:
                    dense()
                    return
                wait(rep_loaded, 2 * REP_LOADS * DMA * (g + 1))
                for p in range(PAIRS):
                    wait(z0_loaded[p], Z0_LOADS * DMA * (g + 1))
                for c in range(CHUNKS):
                    wait(x0b_loaded[c], X0B_LOADS * DMA * (g + 1))
                wait(x0_in_sbuf, 2 * g + 4)
                store_x0()
                wait(x0_stored, 3 * DMA * (g + 2))
                wait(l0_done, 2 * g + 1)
                load_rep(0)
                load_z0(0)
                wait(l0_done, 2 * g + 2)
                load_z0(1)
                wait(l0_products, 4 * g + 6)
                load_rep(1)
                dense()
                for c in range(2):
                    wait(z_ready, ZPG * g + made(2, BLOCKS - 1, c))
                    if (2, BLOCKS - 1, c) in BY_POOL:
                        wait(z_by_pool, len(BY_POOL) * g + by_pool(2))
                    load_x0b(c)
                for c in range(2):
                    wait(z_ready, ZPG * g + made(3, BLOCKS - 1, c))
                    load_x0b(2 + c)
                if lookup is not None:
                    wait(rows_looked_up, M * DMA * (g + 3))
                    if lookup:
                        load_idx(g + 3)

            load_idx(0)
            for dst, src in weight_loads:
                sp.dma_start(dst[:] if dst.shape[0] == P else dst, src).then_inc(weights_loaded, DMA)
            for p in range(PAIRS):
                sp.dma_start(w0_d[M * p:M * p + M, :], w0_diag).then_inc(weights_loaded, DMA)
            sp.dma_start(wt1_s[0:H + D, 1], wt1[P:]).then_inc(weights_loaded, DMA)
            sp.wait_ge(rows_looked_up, M * DMA)
            load_idx(1)
            sp.wait_ge(x0_in_sbuf, 2)
            store_x0()
            sp.wait_ge(x0_stored, 3 * DMA)
            load_rep(0)
            load_z0(0)
            load_z0(1)
            sp.wait_ge(l0_products, 2)
            load_rep(1)
            for c in range(CHUNKS):
                load_x0b(c)
            sp.wait_ge(rows_looked_up, 2 * M * DMA)
            load_idx(2)
            iteration(0, True, True, False)
            with sp.Fori(1, G - 3) as g:
                iteration(g, True, True, True)
            iteration(G - 3, True, False, True)
            iteration(G - 2, True, None, True)
            iteration(G - 1, False, None, True)

        @block.gpsimd
        def _(pool):
            def look_up(fields):
                for m in fields:
                    pool.indirect_dma_start(
                        out=looked_up[:, m * D:(m + 1) * D], out_offset=None, in_=tables[m],
                        in_offset=bass.IndirectOffsetOnAxis(ap=idx[:, m:m + 1], axis=0),
                    ).then_inc(rows_looked_up, DMA)

            def products(g, pair):
                pool.wait_ge(rep_loaded, REP_LOADS * DMA * (2 * g + pair + 1))
                pool.wait_ge(z0_loaded[pair], Z0_LOADS * DMA * (g + 1))
                for c in range(2):
                    chunk = 2 * pair + c
                    nc.gpsimd.tensor_tensor(
                        l0_z[:, chunk], l0_z[:, chunk], l0_rep[:, c].unsqueeze(1).to_broadcast([P, T0, N]), ALU.mult,
                    ).then_inc(l0_products, 1)

            def cin_block(g, s, fresh=False):
                j, chunk = BLOCKS - 1, 2 * (s % PAIRS) + 1
                pool.wait_ge(x0b_loaded[chunk], X0B_LOADS * DMA * (g + 1))
                pool.wait_ge(xk_pool_ready, len(BY_POOL) * g + by_pool(s))
                if not (fresh and s == 0):
                    pool.wait_ge(z_used, UPG * g + BLOCKS * s)
                nc.gpsimd.tensor_tensor(
                    z[:, 2 * j + 1], x0_b[:, chunk, MQ - ZU:MQ],
                    xk_pool[:].unsqueeze(1).to_broadcast([P, ZU, N]), ALU.mult,
                ).then_inc(z_by_pool, 1)

            def iteration(g, front, lookup, fresh=False):
                quarter = M // 4
                cin_block(g, 0, fresh)
                if lookup:
                    pool.wait_ge(idx_loaded, DMA * (g + 3))
                    pool.wait_ge(x0_transposed, g + 2)
                    pool.sem_inc(steps_of_pool, 1)
                    look_up(range(0, 2 * quarter))
                cin_block(g, 1)
                if front:
                    products(g + 1, 0)
                cin_block(g, 2)
                if lookup:
                    look_up(range(2 * quarter, 3 * quarter))
                if front:
                    products(g + 1, 1)
                if lookup:
                    look_up(range(3 * quarter, M))

            nc.gpsimd.memset(ident[:], 0.0).then_inc(ident_zero, 1)
            pool.wait_ge(ident_zero, 1)
            nc.gpsimd.affine_select(
                out=ident[:], in_=ident[:], compare_op=ALU.not_equal, fill=1.0, base=0,
                pattern=[[-1, P]], channel_multiplier=1,
            ).then_inc(ident_ready, 1)
            pool.wait_ge(idx_loaded, DMA)
            look_up(range(M))
            pool.wait_ge(x0_transposed, 1)
            pool.wait_ge(idx_loaded, 2 * DMA)
            look_up(range(M))
            iteration(0, True, True, fresh=True)
            with pool.Fori(1, G - 2) as g:
                iteration(g, True, True)
            iteration(G - 2, True, False)
            iteration(G - 1, False, False)

        @block.tensor
        def _(pe):
            def transposes(g):
                pe.wait_ge(rows_looked_up, M * DMA * (g + 1))
                by_coord = looked_up[:].rearrange("p (mc q) -> p q mc", q=CHUNKS)
                for q in range(CHUNKS):
                    last = nc.tensor.transpose(stage[:, q * P:(q + 1) * P], by_coord[:, q], ident[:])
                last.then_inc(x0_transposed, 1)

            def layer0(g, pair):
                to = acc[:, ACC0[pair]]
                pe.wait_ge(l0_products, 4 * g + 2 * pair + 2)
                for t in range(T0):
                    for c in range(2):
                        nc.tensor.matmul(
                            to[64 * c:64 * c + H], w0_s[:, t], l0_z[:, 2 * pair + c, t], start=(t == 0), stop=False)
                squares = slice(M * pair, M * pair + M)
                for c in range(2):
                    last = nc.tensor.matmul(
                        to[64 * c:64 * c + H], w0_d[squares], l0_sq[squares, c], start=False, stop=True)
                last.then_inc(l0_done, 1)

            def contract(g, s):
                layer, pair = 1 + s // PAIRS, s % PAIRS
                to = acc[:, (ACC0, ACC1, ACC2)[layer][pair]]
                for j in range(BLOCKS):
                    pe.wait_ge(z_ready, ZPG * g + made(s, j, 1))
                    if (s, j, 1) in BY_POOL:
                        pe.wait_ge(z_by_pool, len(BY_POOL) * g + by_pool(s))
                    for u in range(ZU):
                        k = j * ZU + u
                        for c in range(2):
                            last = nc.tensor.matmul(
                                to[64 * c:64 * c + H], w_cin[:, layer - 1, k], z[:, 2 * j + c, u],
                                start=(k == 0), stop=(k == KT - 1),
                            )
                    last.then_inc(z_used, 1)

            def mlp1(g, staged):
                pe.wait_ge(mlp_in_ready, g + 1)
                pe.wait_ge(dense_loaded, DMA * (g + 1))
                pe.wait_ge(x0_in_sbuf, 2 * staged)
                for i in range(F1 // P):
                    cols = slice(i * P, (i + 1) * P)
                    nc.tensor.matmul(stage[:, cols], wt1_s[:, 0, cols], mlp_in[:, 0], start=True, stop=False)
                    last = nc.tensor.matmul(
                        stage[:, cols], wt1_s[0:H + D, 1, cols], mlp_in[0:H + D, 1], start=False, stop=True)
                last.then_inc(h1_done, 1)

            def mlp2(g):
                pe.wait_ge(h1_ready, g + 1)
                for i in range(F2 // P):
                    cols = slice(i * P, (i + 1) * P)
                    for k in range(F1 // P):
                        last = nc.tensor.matmul(stage[:, cols], wt2_s[:, k, cols], h1[:, k], start=(k == 0), stop=(k == F1 // P - 1))
                last.then_inc(h2_done, 1)

            def mlp3(g):
                pe.wait_ge(h2_ready, g + 1)
                for k in range(F2 // P):
                    last = nc.tensor.matmul(stage[0:1, 0:P], wt3_s[:, k:k + 1], h2[:, k], start=(k == 0), stop=(k == F2 // P - 1))
                last.then_inc(y_done, 1)

            def iteration(g, front, mlp):
                if not (isinstance(g, int) and g < 2):
                    pe.wait_ge(y_ready, g - 1)
                if front and mlp:
                    transposes(g + 1)
                if mlp:
                    pe.wait_ge(acc_summed, 6 * g)
                contract(g, 0)
                if front and not mlp:
                    transposes(g + 1)
                pe.wait_ge(xk_ready, XPG * g + 4)
                pe.wait_ge(acc_summed, 6 * g + 1)
                contract(g, 1)
                if mlp:
                    mlp1(g - 1, g + 2 if front else G)
                pe.wait_ge(xk_ready, XPG * g + 8)
                pe.wait_ge(acc_summed, 6 * g + 2)
                contract(g, 2)
                if mlp:
                    mlp2(g - 1)
                if front:
                    pe.wait_ge(xk_ready, XPG * g + 16)
                    pe.wait_ge(acc_summed, 6 * g + 4)
                    layer0(g + 1, 0)
                pe.wait_ge(xk_ready, XPG * g + 12)
                pe.wait_ge(acc_summed, 6 * g + 3)
                contract(g, 3)
                if mlp:
                    mlp3(g - 1)
                if front:
                    pe.wait_ge(acc_summed, 6 * g + 5)
                    layer0(g + 1, 1)

            pe.wait_ge(ident_ready, 1)
            transposes(0)
            pe.wait_ge(w0_ready, 2)
            pe.wait_ge(weights_loaded, WEIGHTS)
            layer0(0, 0)
            layer0(0, 1)
            iteration(0, True, False)
            with pe.Fori(1, G - 1) as g:
                iteration(g, True, True)
            iteration(G - 1, False, True)
            pe.wait_ge(y_ready, G - 1)
            mlp1(G - 1, G)
            mlp2(G - 1)
            mlp3(G - 1)

        @block.scalar
        def _(act):
            def x0_out(g):
                act.wait_ge(x0_transposed, g + 1)
                if not (isinstance(g, int) and g == 0):
                    act.wait_ge(x0_stored, 3 * DMA * g)
                src = stage[:].rearrange("p (q r) -> p q r", q=CHUNKS)
                nc.scalar.activation(x0_t[:], src, ACT.Copy).then_inc(x0_in_sbuf, 1)
                nc.scalar.activation(x0_sq[:], src, ACT.Square).then_inc(x0_in_sbuf, 1)

            def xk_tiles(g, s, bank, wait_source, first=False):
                wait_source()
                for h in range(HH):
                    for c in range(2):
                        slot = 2 * h + c
                        if not first:
                            act.wait_ge(z_ready, ZPG * g + made(s - 1, 2 * h + 1, c))
                        src = acc[64 * c + 32 * h:64 * c + 32 * h + 32, bank]
                        for q in range(4):
                            last = nc.scalar.activation(xk[32 * q:32 * q + 32, slot], src, ACT.Relu)
                        last.then_inc(xk_ready, 1)
                        if (s % LG, BLOCKS - 1, c) in BY_POOL and h == HH - 1:
                            if not first:
                                act.wait_ge(z_by_pool, len(BY_POOL) * g + by_pool(s - 1))
                            for q in range(4):
                                last = nc.scalar.activation(xk_pool[32 * q:32 * q + 32], src, ACT.Relu)
                            last.then_inc(xk_pool_ready, 1)

            def after_layer0(g, pair):
                return lambda: act.wait_ge(l0_done, 2 * g + pair + 1)

            def after_step(g, s):
                return lambda: act.wait_ge(z_used, UPG * g + BLOCKS * (s + 1))

            def cross(g):
                act.wait_ge(zvec_ready, 3 * g + 3)
                if not (isinstance(g, int) and g == 0):
                    act.wait_ge(mlp_in_ready, g)
                for layer, first, tile in mlp_zvec:
                    other = H - first
                    last = nc.scalar.activation(zcross[first:first + H, tile], zvec[other:other + H, layer], ACT.Copy)
                last.then_inc(zcross_ready, 1)

            def h1_out(g):
                act.wait_ge(h1_done, g + 1)
                if not (isinstance(g, int) and g == 0):
                    act.wait_ge(h2_done, g)
                for i in range(F1 // P):
                    last = nc.scalar.activation(h1[:, i], stage[:, i * P:(i + 1) * P], ACT.Relu, bias=bt1_s[:, i:i + 1])
                last.then_inc(h1_ready, 1)

            def h2_out(g):
                act.wait_ge(h2_done, g + 1)
                if not (isinstance(g, int) and g == 0):
                    act.wait_ge(y_done, g)
                for i in range(F2 // P):
                    last = nc.scalar.activation(h2[:, i], stage[:, i * P:(i + 1) * P], ACT.Relu, bias=bt2_s[:, i:i + 1])
                last.then_inc(h2_ready, 1)

            def y_out(g):
                act.wait_ge(y_done, g + 1)
                if not (isinstance(g, int) and g == 0):
                    act.wait_ge(out_stored, DMA * g)
                nc.scalar.activation(y_s[:], stage[0:1, 0:P], ACT.Copy).then_inc(y_ready, 1)
                act.wait_ge(y_ready, g + 1)
                act.dma_start(out[bass.ds(g, 1)].rearrange("g r one -> (g one) r"), y_s[:]).then_inc(out_stored, DMA)

            def iteration(g, front, mlp):
                if front and mlp:
                    x0_out(g + 1)
                xk_tiles(g, 1, ACC0[1], after_layer0(g, 1))
                if front and not mlp:
                    x0_out(g + 1)
                if mlp:
                    cross(g - 1)
                xk_tiles(g, 2, ACC1[0], after_step(g, 0))
                xk_tiles(g, 3, ACC1[1], after_step(g, 1))
                if mlp:
                    h1_out(g - 1)
                if front:
                    xk_tiles(g, 4, ACC0[0], after_layer0(g + 1, 0))
                if mlp:
                    h2_out(g - 1)
                    y_out(g - 1)

            x0_out(0)
            act.wait_ge(weights_loaded, WEIGHTS)
            xk_tiles(0, 0, ACC0[0], after_layer0(0, 0), first=True)
            iteration(0, True, False)
            iteration(1, True, True)
            with act.Fori(2, G - 1) as g:
                iteration(g, True, True)
            iteration(G - 1, False, True)
            cross(G - 1)
            h1_out(G - 1)
            h2_out(G - 1)
            y_out(G - 1)
            act.wait_ge(out_stored, DMA * G)

        @block.vector
        def _(dve):
            def products(g, s, j, c, fresh):
                if (s, j, c) in BY_POOL:
                    return
                chunk, h, m0 = 2 * (s % PAIRS) + c, (j * ZU) // MQ, (j * ZU) % MQ
                if s < PAIRS and j == 0:
                    dve.wait_ge(x0b_loaded[chunk], X0B_LOADS * DMA * (g + 1))
                if j % (BLOCKS // HH) == 0:
                    dve.wait_ge(xk_ready, XPG * g + 2 * HH * s + 2 * h + c + 1)
                if c == 0 and not (fresh and s == 0):
                    dve.wait_ge(z_used, UPG * g + BLOCKS * (s - 1) + j + 1)
                nc.vector.tensor_tensor(
                    z[:, 2 * j + c], x0_b[:, chunk, m0:m0 + ZU],
                    xk[:, 2 * h + c].unsqueeze(1).to_broadcast([P, ZU, N]), ALU.mult,
                ).then_inc(z_ready, 1)

            def add_up(layer, pair, done):
                src = acc[:, (ACC0, ACC1, ACC2)[layer][pair]]
                if pair == 0:
                    ins = nc.vector.tensor_scalar(zsum[:], src, 0.0, None, ALU.max)
                else:
                    dve.wait_ge(acc_summed, done)
                    ins = nc.vector.scalar_tensor_tensor(zsum[:], src, 0.0, zsum[:], ALU.max, ALU.add)
                ins.then_inc(acc_summed, 1)

            def add_coordinates(g, layer):
                dve.wait_ge(acc_summed, 6 * g + 2 * layer + 2)
                nc.vector.tensor_reduce(
                    zvec[:, layer], zsum[:].rearrange("p (c r) -> p r c", c=DC), AX.X, ALU.add,
                ).then_inc(zvec_ready, 1)

            def add_chunks(g):
                dve.wait_ge(zcross_ready, g + 1)
                if not (isinstance(g, int) and g == 0):
                    dve.wait_ge(h1_done, g)
                for layer, first, tile in mlp_zvec:
                    rows = slice(first, first + H)
                    last = nc.vector.tensor_tensor(mlp_in[rows, tile], zvec[rows, layer], zcross[rows, tile], ALU.add)
                last.then_inc(mlp_in_ready, 1)

            def finish(g):
                dve.wait_ge(z_used, UPG * (g + 1))
                add_up(2, 1, 6 * g + 5)
                add_coordinates(g, 2)

            def iteration(g, fresh=False):
                for s in range(LG):
                    for j in range(BLOCKS):
                        for c in range(2):
                            products(g, s, j, c, fresh)
                        if (s, j) == (0, 1):
                            if not fresh:
                                finish(g - 1)
                                dve.wait_ge(zvec_ready, 3 * g)
                            dve.wait_ge(xk_ready, XPG * g + 4)
                            dve.wait_ge(xk_pool_ready, len(BY_POOL) * g + by_pool(0))
                            add_up(0, 0, None)
                        if (s, j) == (1, 0) and not fresh:
                            add_chunks(g - 1)
                        if (s, j) == (1, 1):
                            dve.wait_ge(xk_ready, XPG * g + 8)
                            dve.wait_ge(xk_pool_ready, len(BY_POOL) * g + by_pool(1))
                            add_up(0, 1, 6 * g + 1)
                        if (s, j) == (1, 3):
                            if not fresh:
                                dve.wait_ge(mlp_in_ready, g)
                            add_coordinates(g, 0)
                        if (s, j) == (2, 0):
                            dve.wait_ge(zvec_ready, 3 * g + 1)
                            dve.wait_ge(xk_ready, XPG * g + 12)
                            dve.wait_ge(xk_pool_ready, len(BY_POOL) * g + by_pool(2))
                            add_up(1, 0, None)
                        if (s, j) == (3, 0):
                            dve.wait_ge(xk_ready, XPG * g + 16)
                            add_up(1, 1, 6 * g + 3)
                        if (s, j) == (3, 1):
                            add_coordinates(g, 1)
                        if (s, j) == (3, 2):
                            dve.wait_ge(zvec_ready, 3 * g + 2)
                            dve.wait_ge(z_used, UPG * g + 3 * BLOCKS)
                            add_up(2, 0, None)

            dve.wait_ge(weights_loaded, WEIGHTS)
            nc.vector.tensor_tensor(w0_s[:, 0:T0 - 1], w0_s[:, 0:T0 - 1], w0_t[:, 0:T0 - 1], ALU.add).then_inc(w0_ready, 1)
            nc.vector.tensor_tensor(w0_s[0:96, T0 - 1], w0_s[0:96, T0 - 1], w0_t[0:96, T0 - 1], ALU.add).then_inc(w0_ready, 1)
            for pair in range(PAIRS):
                dve.wait_ge(rep_loaded, REP_LOADS * DMA * (pair + 1))
                dve.wait_ge(z0_loaded[pair], Z0_LOADS * DMA)
                for c in range(2):
                    chunk = 2 * pair + c
                    nc.vector.tensor_tensor(
                        l0_z[:, chunk], l0_z[:, chunk], l0_rep[:, c].unsqueeze(1).to_broadcast([P, T0, N]), ALU.mult,
                    ).then_inc(l0_products, 1)
            dve.wait_ge(w0_ready, 2)
            iteration(0, fresh=True)
            iteration(1)
            with dve.Fori(2, G) as g:
                iteration(g)
            finish(G - 1)
            add_chunks(G - 1)


def kernel(dense_ctx, ids, W_top1, b_top1, W_top2, b_top2, W_top3, L0_rec_W0, L0_rec_W1, L0_rec_W2, **tables):
    import concourse.bacc as bacc
    import numpy as np
    from concourse.bass_utils import run_bass_kernel_spmd

    w0 = np.asarray(L0_rec_W0)
    j, m, t = np.meshgrid(np.arange(4), np.arange(M), np.arange(T0), indexing="ij")
    other = (m + 4 * t + j + 1) % M

    def tiles(w):
        w = np.asarray(w).reshape(MQ, 4, HH, 32, H)
        return np.ascontiguousarray(w.transpose(1, 3, 2, 0, 4).reshape(P, KT, H))

    arrays = {
        "dense_t": np.ascontiguousarray(np.asarray(dense_ctx).reshape(G, P, D).transpose(0, 2, 1)),
        "ids": np.asarray(ids).reshape(G, P, M),
        "w0_a": np.ascontiguousarray(w0[m, other].reshape(P, T0, H)),
        "w0_b": np.ascontiguousarray(w0[other, m].reshape(P, T0, H)),
        "w0_diag": np.ascontiguousarray(w0[np.arange(M), np.arange(M)]),
        "w1": tiles(L0_rec_W1),
        "w2": tiles(L0_rec_W2),
        "wt1": np.asarray(W_top1),
        "bt1": np.ascontiguousarray(np.asarray(b_top1).reshape(F1 // P, P).T),
        "wt2": np.ascontiguousarray(np.asarray(W_top2).reshape(F1 // P, P, F2).transpose(1, 0, 2)),
        "bt2": np.ascontiguousarray(np.asarray(b_top2).reshape(F2 // P, P).T),
        "wt3": np.ascontiguousarray(np.asarray(W_top3).reshape(F2 // P, P).T),
    }
    for f in range(M):
        arrays[f"tbl_{f}"] = np.asarray(tables[f"tbl_{f}"])
    nc = bacc.Bacc("TRN2", target_bir_lowering=False, num_devices=1)
    dram = {
        name: nc.dram_tensor(name, a.shape, mybir.dt.from_np(a.dtype), kind="ExternalInput").ap()
        for name, a in arrays.items()
    }
    out = nc.dram_tensor("y", (G, P, 1), F32, kind="ExternalOutput").ap()
    table_aps = [dram.pop(f"tbl_{f}") for f in range(M)]
    build(nc, tables=table_aps, out=out, **dram)
    r = run_bass_kernel_spmd(nc, [arrays], core_ids=[0])
    return r.results[0]["y"].reshape(B, 1)
```

```python
from contextlib import ExitStack

import concourse.bass as bass
from concourse import mybir

F32 = mybir.dt.float32
BF16 = mybir.dt.bfloat16
I32 = mybir.dt.int32
ALU = mybir.AluOpType
ACT = mybir.ActivationFunctionType
AX = mybir.AxisListType

P = 128
B, M, D, H = 2048, 32, 16, 64
G = B // P
N = 512
DC = N // P
CHUNKS = D // DC
PAIRS = CHUNKS // 2
MQ = M // 4
HH = H // 32
KT = MQ * HH
ZU = 4
BLOCKS = KT // ZU
ZS = 2 * BLOCKS
T0 = 4
XS = 4
LG = 2 * PAIRS
BY_POOL = {(s, BLOCKS - 1, 1) for s in range(3)}
ZPG = LG * ZS - len(BY_POOL)
UPG = LG * BLOCKS
XPG = LG * 2 * HH
ROWS = 2 * M
SQ = M // 2
PARTS = 3
STACK = [(0, 0), (1, 0), (2, 0), (0, 1), (1, 1), (0, 2)]
F1, F2 = 512, 256
DMA = 16

ACC0, ACC1, ACC2 = (0, 1), (2, 0), (1, 2)


def build(nc, dense_t, ids, tables, w0_a, w0_b, w0_squares, w1, w2, wt1, bt1, wt2, bt2, wt3, out):
    x0_dram = nc.dram_tensor("x0_scratch", [ROWS, CHUNKS, N], F32, kind="Internal").ap()
    sq_dram = nc.dram_tensor("squares_scratch", [PARTS, SQ, CHUNKS, N], BF16, kind="Internal").ap()
    ctx = ExitStack()
    with ctx:
        def sb(name, shape, dt=F32):
            return ctx.enter_context(nc.sbuf_tensor(name, shape, dt))

        def sem(name):
            return ctx.enter_context(nc.semaphore(name))

        ident = sb("ident", [P, P])
        idx = sb("idx", [P, M], I32)
        looked_up = sb("looked_up", [P, M * D])
        x0_t = sb("x0_t", [P, N])
        sq_rest = sb("sq_rest", [SQ * CHUNKS, N])
        sq_parts = sb("sq_parts", [SQ * CHUNKS, PARTS, N], BF16)
        x0_b = sb("x0_b", [P, PAIRS, MQ, 2, N])
        xk_pool = sb("xk_pool", [P, N])
        l0_rep = sb("l0_rep", [P, 2, N])
        l0_z = sb("l0_z", [P, PAIRS, T0, 2, N])
        l0_sq = sb("l0_sq", [len(STACK) * SQ, PAIRS, 2, N], BF16)
        z = sb("z", [P, ZS, ZU, N])
        w0_s = sb("w0_s", [P, T0, H])
        w0_t = z[:, 0, 0, 0:T0 * H].rearrange("p (t k) -> p t k", t=T0)
        l0_rep_1 = z[:, ZS - 1, 0:2]
        w_sq = sb("w_sq", [len(STACK) * SQ, H], BF16)
        w_sq_rest = sb("w_sq_rest", [len(STACK) * SQ, H])
        w_sq_parts = sb("w_sq_parts", [len(STACK) * SQ, PARTS, H], BF16)
        w_cin = sb("w_cin", [P, 2, KT, H])
        wt1_s = sb("wt1_s", [P, 2, F1])
        wt2_s = sb("wt2_s", [P, F1 // P, F2])
        wt3_s = sb("wt3_s", [P, F2 // P])
        bt1_s = sb("bt1_s", [P, F1 // P])
        bt2_s = sb("bt2_s", [P, F2 // P])
        zsum = sb("zsum", [P, DC * P])
        zvec = sb("zvec", [P, 3, P])
        zcross = sb("zcross", [P, 2, P])
        mlp_in = sb("mlp_in", [P, 2, P])
        mlp_zvec = [(0, 0, 0), (1, 64, 0), (2, 0, 1)]
        dense_s = mlp_in[H:H + D, 1]
        h1 = sb("h1", [P, F1 // P, P])
        h2 = sb("h2", [P, F2 // P, P])
        y_s = sb("y_s", [1, P])

        acc = ctx.enter_context(nc.psum_tensor("acc", [P, 3, N], F32))
        xk = ctx.enter_context(nc.psum_tensor("xk", [P, XS, N], F32))
        stage = ctx.enter_context(nc.psum_tensor("stage", [P, N], F32))

        weights_loaded = sem("weights_loaded")
        ident_zero = sem("ident_zero")
        ident_ready = sem("ident_ready")
        w0_ready = sem("w0_ready")
        idx_loaded = sem("idx_loaded")
        rows_looked_up = sem("rows_looked_up")
        x0_transposed = sem("x0_transposed")
        x0_in_sbuf = sem("x0_in_sbuf")
        x0_stored = sem("x0_stored")
        sq_first = sem("sq_first")
        sq_second = sem("sq_second")
        sq_left = sem("sq_left")
        sq_third = sem("sq_third")
        sq_stored = sem("sq_stored")
        sq_loaded = [sem(f"sq_loaded{p}") for p in range(PAIRS)]
        w_sq_steps = sem("w_sq_steps")
        w_sq_loaded = sem("w_sq_loaded")
        z0_loaded = [sem(f"z0_loaded{p}") for p in range(PAIRS)]
        rep_loaded = [sem(f"rep_loaded{p}") for p in range(PAIRS)]
        x0b_loaded = [[sem(f"x0b_loaded{p}_{i}") for i in range(2)] for p in range(PAIRS)]
        l0_products = sem("l0_products")
        l0_done = sem("l0_done")
        xk_ready = sem("xk_ready")
        xk_pool_ready = sem("xk_pool_ready")
        z_by_pool = sem("z_by_pool")
        z_ready = sem("z_ready")
        z_used = sem("z_used")
        acc0_taken = sem("acc0_taken")
        acc1_taken = sem("acc1_taken")
        zvec_ready = sem("zvec_ready")
        zcross_ready = sem("zcross_ready")
        mlp_in_ready = sem("mlp_in_ready")
        dense_loaded = sem("dense_loaded")
        h1_done = sem("h1_done")
        h1_ready = sem("h1_ready")
        h2_done = sem("h2_done")
        h2_ready = sem("h2_ready")
        y_done = sem("y_done")
        y_ready = sem("y_ready")
        out_stored = sem("out_stored")
        steps_of_sync = sem("steps_of_sync")
        steps_of_pool = sem("steps_of_pool")

        weight_loads = [
            (w0_s, w0_a), (w0_t, w0_b), (w_sq_rest, w0_squares), (w_cin[:, 0], w1), (w_cin[:, 1], w2),
            (wt1_s[:, 0], wt1[0:P]), (wt2_s, wt2), (wt3_s, wt3), (bt1_s, bt1), (bt2_s, bt2),
        ]
        WEIGHTS = DMA * (len(weight_loads) + 1)
        Z0_LOADS = 6
        REP_LOADS = 4
        X0B_LOADS = 4

        def made(s, j, c):
            at = (s, j, c)
            return sum(b <= at and b not in BY_POOL for b in
                       [(i, k, e) for i in range(LG) for k in range(BLOCKS) for e in range(2)])

        def by_pool(s):
            return sum(b[0] <= s for b in BY_POOL)

        block = ctx.enter_context(nc.Block())

        @block.sync
        def _(sp):
            def load_idx(g):
                sp.dma_start(idx[:], ids[bass.ds(g, 1)].rearrange("g r m -> (g r) m")).then_inc(idx_loaded, DMA)

            def store_x0():
                for first in (0, M):
                    dst = x0_dram[first:first + M].rearrange("m c n -> (m c) n")
                    sp.dma_start(dst, x0_t[:]).then_inc(x0_stored, DMA)

            def store_squares():
                sp.dma_start(sq_dram.rearrange("p m c n -> (m c) p n"), sq_parts[:]).then_inc(sq_stored, DMA)

            def load_squares():
                for p in range(PAIRS):
                    for w in range(PARTS):
                        first, count = STACK.index((0, w)), PARTS - w
                        src = sq_dram[0:count, :, 2 * p:2 * p + 2].rearrange("p m c n -> (p m) c n")
                        dst = l0_sq[SQ * first:SQ * (first + count), p]
                        sp.dma_start(dst, src).then_inc(sq_loaded[p], DMA)

            def load_z0(pair):
                rows = x0_dram[:, 2 * pair:2 * pair + 2]
                row = CHUNKS * N
                for j in range(4):
                    shifted = rows[j + 1:j + 1 + M]
                    tiles = T0 if j < 3 else T0 - 1
                    src = bass.AP(shifted.tensor, shifted.offset, [[row, M], [4 * row, tiles], [1, 2 * N]])
                    dst = l0_z[32 * j:32 * j + 32, pair, 0:tiles].rearrange("p t c n -> p t (c n)")
                    sp.dma_start(dst, src).then_inc(z0_loaded[pair], DMA)
                for first in (96, 96 + SQ):
                    sp.dma_start(l0_z[first:first + SQ, pair, T0 - 1], rows[SQ:M]).then_inc(z0_loaded[pair], DMA)

            def load_rep(pair, to=l0_rep):
                for j in range(4):
                    sp.dma_start(to[32 * j:32 * j + 32], x0_dram[0:M, 2 * pair:2 * pair + 2]).then_inc(rep_loaded[pair], DMA)

            def load_x0b(pair):
                half = MQ // 2
                for i in range(2):
                    for j in range(4):
                        row = 4 * half * i + j
                        first = x0_dram[row:row + 1, 2 * pair:2 * pair + 2]
                        src = bass.AP(first.tensor, first.offset, [[0, 32], [4 * CHUNKS * N, half], [1, 2 * N]])
                        dst = x0_b[32 * j:32 * j + 32, pair, half * i:half * (i + 1)].rearrange("p m c n -> p m (c n)")
                        sp.dma_start(dst, src).then_inc(x0b_loaded[pair][i], DMA)

            def load_dense(g):
                sp.dma_start(dense_s, dense_t[bass.ds(g, 1)].rearrange("g d r -> (g d) r")).then_inc(dense_loaded, DMA)

            def iteration(g, front, lookup, mlp):
                def wait(semaphore, value):
                    sp.wait_ge(semaphore, value)
                    sp.sem_inc(steps_of_sync, 1)

                def dense():
                    if mlp:
                        wait(h1_done, g)
                    load_dense(g)

                if not front:
                    dense()
                    return
                for p in range(PAIRS):
                    wait(rep_loaded[p], REP_LOADS * DMA * (g + 1))
                    wait(z0_loaded[p], Z0_LOADS * DMA * (g + 1))
                    for i in range(2):
                        wait(x0b_loaded[p][i], X0B_LOADS * DMA * (g + 1))
                wait(x0_in_sbuf, g + 2)
                store_x0()
                wait(x0_stored, 2 * DMA * (g + 2))
                wait(l0_done, 2 * g + 1)
                load_rep(0)
                load_z0(0)
                wait(l0_done, 2 * g + 2)
                load_z0(1)
                wait(sq_third, g + 2)
                for p in range(PAIRS):
                    wait(sq_loaded[p], PARTS * DMA * (g + 1))
                store_squares()
                wait(sq_stored, DMA * (g + 2))
                load_squares()
                wait(l0_products, 4 * g + 6)
                load_rep(1)
                dense()
                for p in range(PAIRS):
                    wait(z_ready, ZPG * g + made(2 + p, BLOCKS - 1, 1))
                    if (2 + p, BLOCKS - 1, 1) in BY_POOL:
                        wait(z_by_pool, len(BY_POOL) * g + by_pool(2 + p))
                    load_x0b(p)
                if lookup is not None:
                    wait(rows_looked_up, M * DMA * (g + 3))
                    if lookup:
                        load_idx(g + 3)

            load_idx(0)
            for dst, src in weight_loads:
                sp.dma_start(dst[:], src).then_inc(weights_loaded, DMA)
            sp.dma_start(wt1_s[0:H + D, 1], wt1[P:]).then_inc(weights_loaded, DMA)
            sp.wait_ge(rows_looked_up, M * DMA)
            load_idx(1)
            sp.wait_ge(w_sq_steps, 4)
            for w in range(PARTS):
                rows = slice(SQ * STACK.index((0, w)), SQ * (STACK.index((0, w)) + PARTS - w))
                sp.dma_start(w_sq[rows], w_sq_parts[rows, w]).then_inc(w_sq_loaded, DMA)
            sp.wait_ge(x0_in_sbuf, 1)
            store_x0()
            sp.wait_ge(x0_stored, 2 * DMA)
            load_rep(0)
            load_z0(0)
            sp.wait_ge(sq_third, 1)
            store_squares()
            load_rep(1, l0_rep_1)
            load_z0(1)
            sp.wait_ge(sq_stored, DMA)
            load_squares()
            load_x0b(0)
            sp.wait_ge(rows_looked_up, 2 * M * DMA)
            load_idx(2)
            load_x0b(1)
            iteration(0, True, True, False)
            with sp.Fori(1, G - 3) as g:
                iteration(g, True, True, True)
            iteration(G - 3, True, False, True)
            iteration(G - 2, True, None, True)
            iteration(G - 1, False, None, True)

        @block.gpsimd
        def _(pool):
            def look_up(fields):
                for m in fields:
                    pool.indirect_dma_start(
                        out=looked_up[:, m * D:(m + 1) * D], out_offset=None, in_=tables[m],
                        in_offset=bass.IndirectOffsetOnAxis(ap=idx[:, m:m + 1], axis=0),
                    ).then_inc(rows_looked_up, DMA)

            def products(g, pair):
                pool.wait_ge(rep_loaded[pair], REP_LOADS * DMA * (g + 1))
                pool.wait_ge(z0_loaded[pair], Z0_LOADS * DMA * (g + 1))
                for c in range(2):
                    nc.gpsimd.tensor_tensor(
                        l0_z[:, pair, :, c], l0_z[:, pair, :, c],
                        l0_rep[:, c].unsqueeze(1).to_broadcast([P, T0, N]), ALU.mult,
                    ).then_inc(l0_products, 1)

            def cin_block(g, s, fresh=False):
                j, pair = BLOCKS - 1, s % PAIRS
                pool.wait_ge(x0b_loaded[pair][1], X0B_LOADS * DMA * (g + 1))
                pool.wait_ge(xk_pool_ready, len(BY_POOL) * g + by_pool(s))
                if not (fresh and s == 0):
                    pool.wait_ge(z_used, UPG * g + BLOCKS * s)
                nc.gpsimd.tensor_tensor(
                    z[:, 2 * j + 1], x0_b[:, pair, MQ - ZU:MQ, 1],
                    xk_pool[:].unsqueeze(1).to_broadcast([P, ZU, N]), ALU.mult,
                ).then_inc(z_by_pool, 1)

            def iteration(g, front, lookup, fresh=False):
                cin_block(g, 0, fresh)
                if lookup:
                    pool.wait_ge(idx_loaded, DMA * (g + 3))
                    pool.wait_ge(x0_transposed, g + 2)
                    pool.sem_inc(steps_of_pool, 1)
                    look_up(range(0, M // 2))
                cin_block(g, 1)
                if front:
                    products(g + 1, 0)
                cin_block(g, 2)
                if lookup:
                    look_up(range(M // 2, M))
                if front:
                    products(g + 1, 1)

            nc.gpsimd.memset(ident[:], 0.0).then_inc(ident_zero, 1)
            pool.wait_ge(ident_zero, 1)
            nc.gpsimd.affine_select(
                out=ident[:], in_=ident[:], compare_op=ALU.not_equal, fill=1.0, base=0,
                pattern=[[-1, P]], channel_multiplier=1,
            ).then_inc(ident_ready, 1)
            pool.wait_ge(idx_loaded, DMA)
            look_up(range(M))
            pool.wait_ge(x0_transposed, 1)
            pool.wait_ge(idx_loaded, 2 * DMA)
            look_up(range(M))
            pool.wait_ge(l0_products, 4)
            iteration(0, True, True, fresh=True)
            with pool.Fori(1, G - 2) as g:
                iteration(g, True, True)
            iteration(G - 2, True, False)
            iteration(G - 1, False, False)

        @block.tensor
        def _(pe):
            def transposes(g):
                pe.wait_ge(rows_looked_up, M * DMA * (g + 1))
                by_coord = looked_up[:].rearrange("p (mc q) -> p q mc", q=DC)
                for q in range(DC):
                    last = nc.tensor.transpose(stage[:, q * P:(q + 1) * P], by_coord[:, q], ident[:])
                last.then_inc(x0_transposed, 1)

            def layer0(g, pair):
                to = acc[:, ACC0[pair]]
                pe.wait_ge(l0_products, 4 * g + 2 * pair + 2)
                for t in range(T0):
                    for c in range(2):
                        nc.tensor.matmul(
                            to[64 * c:64 * c + H], w0_s[:, t], l0_z[:, pair, t, c], start=(t == 0), stop=False)
                pe.wait_ge(sq_loaded[pair], PARTS * DMA * (g + 1))
                for c in range(2):
                    last = nc.tensor.matmul(
                        to[64 * c:64 * c + H], w_sq[:], l0_sq[:, pair, c], start=False, stop=True)
                last.then_inc(l0_done, 1)

            def contract(g, s):
                layer, pair = 1 + s // PAIRS, s % PAIRS
                to = acc[:, (ACC0, ACC1, ACC2)[layer][pair]]
                for j in range(BLOCKS):
                    pe.wait_ge(z_ready, ZPG * g + made(s, j, 1))
                    if (s, j, 1) in BY_POOL:
                        pe.wait_ge(z_by_pool, len(BY_POOL) * g + by_pool(s))
                    for u in range(ZU):
                        k = j * ZU + u
                        for c in range(2):
                            last = nc.tensor.matmul(
                                to[64 * c:64 * c + H], w_cin[:, layer - 1, k], z[:, 2 * j + c, u],
                                start=(k == 0), stop=(k == KT - 1),
                            )
                    last.then_inc(z_used, 1)

            def mlp1(g, staged):
                pe.wait_ge(mlp_in_ready, g + 1)
                pe.wait_ge(dense_loaded, DMA * (g + 1))
                pe.wait_ge(x0_in_sbuf, staged)
                pe.wait_ge(sq_first, staged)
                for i in range(F1 // P):
                    cols = slice(i * P, (i + 1) * P)
                    nc.tensor.matmul(stage[:, cols], wt1_s[:, 0, cols], mlp_in[:, 0], start=True, stop=False)
                    last = nc.tensor.matmul(
                        stage[:, cols], wt1_s[0:H + D, 1, cols], mlp_in[0:H + D, 1], start=False, stop=True)
                last.then_inc(h1_done, 1)

            def mlp2(g):
                pe.wait_ge(h1_ready, g + 1)
                for i in range(F2 // P):
                    cols = slice(i * P, (i + 1) * P)
                    for k in range(F1 // P):
                        last = nc.tensor.matmul(
                            stage[:, cols], wt2_s[:, k, cols], h1[:, k], start=(k == 0), stop=(k == F1 // P - 1))
                last.then_inc(h2_done, 1)

            def mlp3(g):
                pe.wait_ge(h2_ready, g + 1)
                for k in range(F2 // P):
                    last = nc.tensor.matmul(
                        stage[0:1, 0:P], wt3_s[:, k:k + 1], h2[:, k], start=(k == 0), stop=(k == F2 // P - 1))
                last.then_inc(y_done, 1)

            def iteration(g, front, mlp):
                if not (isinstance(g, int) and g < 2):
                    pe.wait_ge(y_ready, g - 1)
                if front:
                    transposes(g + 1)
                if mlp:
                    pe.wait_ge(acc1_taken, 3 * g)
                contract(g, 0)
                pe.wait_ge(xk_ready, XPG * g + 4)
                pe.wait_ge(acc0_taken, 3 * g + 1)
                contract(g, 1)
                if mlp:
                    mlp1(g - 1, g + 2 if front else G)
                pe.wait_ge(xk_ready, XPG * g + 8)
                pe.wait_ge(acc1_taken, 3 * g + 1)
                contract(g, 2)
                if mlp:
                    mlp2(g - 1)
                if front:
                    pe.wait_ge(xk_ready, XPG * g + 16)
                    pe.wait_ge(acc1_taken, 3 * g + 2)
                    layer0(g + 1, 0)
                pe.wait_ge(xk_ready, XPG * g + 12)
                pe.wait_ge(acc0_taken, 3 * g + 2)
                contract(g, 3)
                if mlp:
                    mlp3(g - 1)
                if front:
                    pe.wait_ge(acc0_taken, 3 * g + 3)
                    layer0(g + 1, 1)

            pe.wait_ge(ident_ready, 1)
            transposes(0)
            pe.wait_ge(w0_ready, 2)
            pe.wait_ge(w_sq_loaded, PARTS * DMA)
            pe.wait_ge(weights_loaded, WEIGHTS)
            layer0(0, 0)
            layer0(0, 1)
            iteration(0, True, False)
            with pe.Fori(1, G - 1) as g:
                iteration(g, True, True)
            iteration(G - 1, False, True)
            pe.wait_ge(y_ready, G - 1)
            mlp1(G - 1, G)
            mlp2(G - 1)
            mlp3(G - 1)

        @block.scalar
        def _(act):
            def x0_out(g):
                act.wait_ge(x0_transposed, g + 1)
                if not (isinstance(g, int) and g == 0):
                    act.wait_ge(x0_stored, 2 * DMA * g)
                    act.wait_ge(sq_stored, DMA * g)
                nc.scalar.activation(x0_t[:], stage[:], ACT.Copy).then_inc(x0_in_sbuf, 1)
                some = stage[0:SQ * CHUNKS]
                nc.scalar.activation(sq_rest[:], some, ACT.Square)
                nc.scalar.activation(sq_parts[:, 0], some, ACT.Square).then_inc(sq_first, 1)

            def second_part(g):
                act.wait_ge(sq_left, g + 1)
                nc.scalar.activation(sq_parts[:, 1], sq_rest[:], ACT.Copy).then_inc(sq_second, 1)

            def xk_tiles(g, s, bank, wait_source, first=False):
                wait_source()
                for h in range(HH):
                    for c in range(2):
                        slot = 2 * h + c
                        if not first:
                            act.wait_ge(z_ready, ZPG * g + made(s - 1, 2 * h + 1, c))
                        src = acc[64 * c + 32 * h:64 * c + 32 * h + 32, bank]
                        for q in range(4):
                            last = nc.scalar.activation(xk[32 * q:32 * q + 32, slot], src, ACT.Relu)
                        last.then_inc(xk_ready, 1)
                        if (s % LG, BLOCKS - 1, c) in BY_POOL and h == HH - 1:
                            if not first:
                                act.wait_ge(z_by_pool, len(BY_POOL) * g + by_pool(s - 1))
                            for q in range(4):
                                last = nc.scalar.activation(xk_pool[32 * q:32 * q + 32], src, ACT.Relu)
                            last.then_inc(xk_pool_ready, 1)

            def after_layer0(g, pair):
                return lambda: act.wait_ge(l0_done, 2 * g + pair + 1)

            def after_step(g, s):
                return lambda: act.wait_ge(z_used, UPG * g + BLOCKS * (s + 1))

            def take(g, layer):
                if not (isinstance(g, int) and g == 0 and layer == 0):
                    act.wait_ge(zvec_ready, 3 * g + layer)
                nc.scalar.activation(zsum[:], acc[:, (ACC0, ACC1, ACC2)[layer][0]], ACT.Relu).then_inc(acc0_taken, 1)

            def cross(g):
                act.wait_ge(zvec_ready, 3 * g + 3)
                if not (isinstance(g, int) and g == 0):
                    act.wait_ge(mlp_in_ready, g)
                for layer, first, tile in mlp_zvec:
                    other = H - first
                    last = nc.scalar.activation(zcross[first:first + H, tile], zvec[other:other + H, layer], ACT.Copy)
                last.then_inc(zcross_ready, 1)

            def h1_out(g):
                act.wait_ge(h1_done, g + 1)
                if not (isinstance(g, int) and g == 0):
                    act.wait_ge(h2_done, g)
                for i in range(F1 // P):
                    last = nc.scalar.activation(h1[:, i], stage[:, i * P:(i + 1) * P], ACT.Relu, bias=bt1_s[:, i:i + 1])
                last.then_inc(h1_ready, 1)

            def h2_out(g):
                act.wait_ge(h2_done, g + 1)
                if not (isinstance(g, int) and g == 0):
                    act.wait_ge(y_done, g)
                for i in range(F2 // P):
                    last = nc.scalar.activation(h2[:, i], stage[:, i * P:(i + 1) * P], ACT.Relu, bias=bt2_s[:, i:i + 1])
                last.then_inc(h2_ready, 1)

            def y_out(g):
                act.wait_ge(y_done, g + 1)
                if not (isinstance(g, int) and g == 0):
                    act.wait_ge(out_stored, DMA * g)
                nc.scalar.activation(y_s[:], stage[0:1, 0:P], ACT.Copy).then_inc(y_ready, 1)
                act.wait_ge(y_ready, g + 1)
                act.dma_start(out[bass.ds(g, 1)].rearrange("g r one -> (g one) r"), y_s[:]).then_inc(out_stored, DMA)

            def iteration(g, front, mlp):
                if front:
                    x0_out(g + 1)
                xk_tiles(g, 1, ACC0[1], after_layer0(g, 1))
                take(g, 0)
                if mlp:
                    cross(g - 1)
                if front:
                    second_part(g + 1)
                xk_tiles(g, 2, ACC1[0], after_step(g, 0))
                take(g, 1)
                xk_tiles(g, 3, ACC1[1], after_step(g, 1))
                if mlp:
                    h1_out(g - 1)
                if front:
                    xk_tiles(g, 4, ACC0[0], after_layer0(g + 1, 0))
                act.wait_ge(z_used, UPG * g + 3 * BLOCKS)
                take(g, 2)
                if mlp:
                    h2_out(g - 1)
                    y_out(g - 1)

            x0_out(0)
            second_part(0)
            act.wait_ge(weights_loaded, WEIGHTS)
            xk_tiles(0, 0, ACC0[0], after_layer0(0, 0), first=True)
            iteration(0, True, False)
            iteration(1, True, True)
            with act.Fori(2, G - 1) as g:
                iteration(g, True, True)
            iteration(G - 1, False, True)
            cross(G - 1)
            h1_out(G - 1)
            h2_out(G - 1)
            y_out(G - 1)
            act.wait_ge(out_stored, DMA * G)

        @block.vector
        def _(dve):
            def products(g, s, j, c, fresh):
                if (s, j, c) in BY_POOL:
                    return
                pair, h, m0 = s % PAIRS, (j * ZU) // MQ, (j * ZU) % MQ
                if s < PAIRS and c == 0 and j < 2:
                    dve.wait_ge(x0b_loaded[pair][j], X0B_LOADS * DMA * (g + 1))
                if j % (BLOCKS // HH) == 0:
                    dve.wait_ge(xk_ready, XPG * g + 2 * HH * s + 2 * h + c + 1)
                if c == 0 and not (fresh and s == 0):
                    dve.wait_ge(z_used, UPG * g + BLOCKS * (s - 1) + j + 1)
                nc.vector.tensor_tensor(
                    z[:, 2 * j + c], x0_b[:, pair, m0:m0 + ZU, c],
                    xk[:, 2 * h + c].unsqueeze(1).to_broadcast([P, ZU, N]), ALU.mult,
                ).then_inc(z_ready, 1)

            def add_up(g, layer):
                dve.wait_ge(acc0_taken, 3 * g + layer + 1)
                nc.vector.scalar_tensor_tensor(
                    zsum[:], acc[:, (ACC0, ACC1, ACC2)[layer][1]], 0.0, zsum[:], ALU.max, ALU.add,
                ).then_inc(acc1_taken, 1)

            def add_coordinates(g, layer):
                dve.wait_ge(acc1_taken, 3 * g + layer + 1)
                nc.vector.tensor_reduce(
                    zvec[:, layer], zsum[:].rearrange("p (c r) -> p r c", c=DC), AX.X, ALU.add,
                ).then_inc(zvec_ready, 1)

            def add_chunks(g):
                dve.wait_ge(zcross_ready, g + 1)
                if not (isinstance(g, int) and g == 0):
                    dve.wait_ge(h1_done, g)
                for layer, first, tile in mlp_zvec:
                    rows = slice(first, first + H)
                    last = nc.vector.tensor_tensor(mlp_in[rows, tile], zvec[rows, layer], zcross[rows, tile], ALU.add)
                last.then_inc(mlp_in_ready, 1)

            def what_is_left(g):
                dve.wait_ge(sq_first, g + 1)
                nc.vector.tensor_tensor(sq_rest[:], sq_rest[:], sq_parts[:, 0], ALU.subtract).then_inc(sq_left, 1)

            def third_part(g):
                dve.wait_ge(sq_second, g + 1)
                nc.vector.tensor_tensor(sq_parts[:, 2], sq_rest[:], sq_parts[:, 1], ALU.subtract).then_inc(sq_third, 1)

            def finish(g):
                dve.wait_ge(z_used, UPG * (g + 1))
                add_up(g, 2)
                add_coordinates(g, 2)

            def iteration(g, fresh=False, front=True):
                for s in range(LG):
                    for j in range(BLOCKS):
                        for c in range(2):
                            products(g, s, j, c, fresh)
                        if (s, j) == (0, 1) and not fresh:
                            finish(g - 1)
                        if (s, j) == (0 if not fresh else 1, 3) and front:
                            what_is_left(g + 1)
                        if (s, j) == (1, 1):
                            dve.wait_ge(xk_ready, XPG * g + 8)
                            dve.wait_ge(xk_pool_ready, len(BY_POOL) * g + by_pool(1))
                            add_up(g, 0)
                        if (s, j) == (1, 2) and not fresh:
                            add_chunks(g - 1)
                        if (s, j) == (1, 3):
                            if not fresh:
                                dve.wait_ge(mlp_in_ready, g)
                            add_coordinates(g, 0)
                        if (s, j) == (2, 0) and front:
                            third_part(g + 1)
                        if (s, j) == (3, 0):
                            dve.wait_ge(xk_ready, XPG * g + 16)
                            add_up(g, 1)
                        if (s, j) == (3, 1):
                            add_coordinates(g, 1)

            dve.wait_ge(weights_loaded, WEIGHTS)
            nc.vector.tensor_tensor(w0_s[:, 0:T0 - 1], w0_s[:, 0:T0 - 1], w0_t[:, 0:T0 - 1], ALU.add).then_inc(w0_ready, 1)
            pairs = slice(0, P - SQ)
            nc.vector.tensor_tensor(
                w0_s[pairs, T0 - 1], w0_s[pairs, T0 - 1], w0_t[pairs, T0 - 1], ALU.add).then_inc(w0_ready, 1)
            nc.vector.tensor_copy(w_sq_parts[:, 0], w_sq_rest[:]).then_inc(w_sq_steps, 1)
            dve.wait_ge(w_sq_steps, 1)
            nc.vector.tensor_tensor(w_sq_rest[:], w_sq_rest[:], w_sq_parts[:, 0], ALU.subtract).then_inc(w_sq_steps, 1)
            dve.wait_ge(w_sq_steps, 2)
            nc.vector.tensor_copy(w_sq_parts[:, 1], w_sq_rest[:]).then_inc(w_sq_steps, 1)
            dve.wait_ge(w_sq_steps, 3)
            nc.vector.tensor_tensor(w_sq_parts[:, 2], w_sq_rest[:], w_sq_parts[:, 1], ALU.subtract).then_inc(w_sq_steps, 1)
            what_is_left(0)
            third_part(0)
            for pair, replicated in enumerate((l0_rep, l0_rep_1)):
                dve.wait_ge(rep_loaded[pair], REP_LOADS * DMA)
                dve.wait_ge(z0_loaded[pair], Z0_LOADS * DMA)
                for c in range(2):
                    nc.vector.tensor_tensor(
                        l0_z[:, pair, :, c], l0_z[:, pair, :, c],
                        replicated[:, c].unsqueeze(1).to_broadcast([P, T0, N]), ALU.mult,
                    ).then_inc(l0_products, 1)
            dve.wait_ge(w0_ready, 2)
            iteration(0, fresh=True)
            iteration(1)
            with dve.Fori(2, G - 1) as g:
                iteration(g)
            iteration(G - 1, front=False)
            finish(G - 1)
            add_chunks(G - 1)


def kernel(dense_ctx, ids, W_top1, b_top1, W_top2, b_top2, W_top3, L0_rec_W0, L0_rec_W1, L0_rec_W2, **tables):
    import concourse.bacc as bacc
    import numpy as np
    from concourse.bass_utils import run_bass_kernel_spmd

    w0 = np.asarray(L0_rec_W0)
    j, m, t = np.meshgrid(np.arange(4), np.arange(M), np.arange(T0), indexing="ij")
    other = (m + 4 * t + j + 1) % M
    other = np.where((other == (m + M // 2) % M) & (m >= SQ), m, other)
    squares = np.tile(np.arange(SQ), len(STACK))

    def tiles(w):
        w = np.asarray(w).reshape(MQ, 4, HH, 32, H)
        return np.ascontiguousarray(w.transpose(1, 3, 2, 0, 4).reshape(P, KT, H))

    arrays = {
        "dense_t": np.ascontiguousarray(np.asarray(dense_ctx).reshape(G, P, D).transpose(0, 2, 1)),
        "ids": np.asarray(ids).reshape(G, P, M),
        "w0_a": np.ascontiguousarray(w0[m, other].reshape(P, T0, H)),
        "w0_b": np.ascontiguousarray(w0[other, m].reshape(P, T0, H)),
        "w0_squares": np.ascontiguousarray(w0[squares, squares]),
        "w1": tiles(L0_rec_W1),
        "w2": tiles(L0_rec_W2),
        "wt1": np.asarray(W_top1),
        "bt1": np.ascontiguousarray(np.asarray(b_top1).reshape(F1 // P, P).T),
        "wt2": np.ascontiguousarray(np.asarray(W_top2).reshape(F1 // P, P, F2).transpose(1, 0, 2)),
        "bt2": np.ascontiguousarray(np.asarray(b_top2).reshape(F2 // P, P).T),
        "wt3": np.ascontiguousarray(np.asarray(W_top3).reshape(F2 // P, P).T),
    }
    for f in range(M):
        arrays[f"tbl_{f}"] = np.asarray(tables[f"tbl_{f}"])
    nc = bacc.Bacc("TRN2", target_bir_lowering=False, num_devices=1)
    dram = {
        name: nc.dram_tensor(name, a.shape, mybir.dt.from_np(a.dtype), kind="ExternalInput").ap()
        for name, a in arrays.items()
    }
    out = nc.dram_tensor("y", (G, P, 1), F32, kind="ExternalOutput").ap()
    table_aps = [dram.pop(f"tbl_{f}") for f in range(M)]
    build(nc, tables=table_aps, out=out, **dram)
    r = run_bass_kernel_spmd(nc, [arrays], core_ids=[0])
    return r.results[0]["y"].reshape(B, 1)
```
